# Optimizing a Trainium2 kernel written in Bass

```python
import numpy as np
import jax
import jax.numpy as jnp

def _softmax(x, axis=-1):
    return jax.nn.softmax(x, axis=axis)

def _gelu(x):
    return jax.nn.gelu(x, approximate=True)

def _silu(x):
    return jax.nn.silu(x)

def _sigmoid(x):
    return jax.nn.sigmoid(x)

def _layernorm(x, axis=-1, eps=1e-05):
    m = jnp.mean(x, axis=axis, keepdims=True)
    v = jnp.var(x, axis=axis, keepdims=True)
    return (x - m) / jnp.sqrt(v + eps)

def _scatter_add(tgt, idx, src, axis=0):
    return tgt.at[idx].add(src)

def _segment_sum(src, seg, n):
    return jax.ops.segment_sum(src, seg, n)
kernel_name = 'mk_vit_tower_cls_d2_tok_img1024_r4_f31f1c'

def setup_inputs(seed: int=0):
    np.random.seed(seed)
    _w = jnp.asarray

    def _rec_inputs():
        import jax
        import jax.numpy as jnp
        _rk = jax.random.key(seed)
        x = -0.00016672 + 0.999947 * jax.random.normal(jax.random.fold_in(_rk, 1), (16, 3, 96, 96), jnp.float32)
        cls_tok = 0.02 * jax.random.normal(jax.random.fold_in(_rk, 5), (1, 1, 256), jnp.float32)
        return (x, cls_tok)
    x, cls_tok = _rec_inputs()

    def _L0_tok_setup():
        import jax, jax.numpy as jnp
        import numpy as np
        B, C, H, W = (64, 3, 96, 96)
        P = 16
        NP = H // P * (W // P)
        PD = C * P * P
        ED = 256
        NCLS = 1

        def _layernorm(x, g, b, eps=1e-05):
            mu = jnp.mean(x, axis=-1, keepdims=True)
            var = jnp.mean(jnp.square(x - mu), axis=-1, keepdims=True)
            return (x - mu) * jax.lax.rsqrt(var + eps) * g + b
        key = jax.random.key(seed)
        ks = jax.random.split(key, 8)
        x = jax.random.normal(ks[0], (B, C, H, W), dtype=jnp.float32)
        ln1_g = jnp.ones((PD,), jnp.float32)
        ln1_b = jnp.zeros((PD,), jnp.float32)
        W_proj = jax.random.normal(ks[1], (PD, ED), jnp.float32) / np.sqrt(PD)
        b_proj = jnp.zeros((ED,), jnp.float32)
        ln2_g = jnp.ones((ED,), jnp.float32)
        ln2_b = jnp.zeros((ED,), jnp.float32)
        cls_token = jax.random.normal(ks[2], (1, NCLS, ED), jnp.float32)
        pos_emb = jax.random.normal(ks[3], (1, NP + NCLS, ED), jnp.float32)
        return {'x': x, 'ln1_g': ln1_g, 'ln1_b': ln1_b, 'W_proj': W_proj, 'b_proj': b_proj, 'ln2_g': ln2_g, 'ln2_b': ln2_b, 'cls_token': cls_token, 'pos_emb': pos_emb}
    _L0_tok_all = _L0_tok_setup()
    _L0_tok_in = {k: v for k, v in _L0_tok_all.items() if k in ('ln1_g', 'ln1_b', 'W_proj', 'b_proj', 'ln2_g', 'ln2_b', 'cls_token', 'pos_emb')}
    del _L0_tok_all

    def _L0_attn_setup():
        import jax, jax.numpy as jnp
        import numpy as np
        D_MODEL = 256
        NHEAD = 16
        HEAD_DIM = D_MODEL // NHEAD
        SCALE = HEAD_DIM ** (-0.5)
        EPS_LN = 1e-05
        key = jax.random.key(seed)
        ks = jax.random.split(key, 7)
        B, T, D = (2, 512, D_MODEL)
        x = jax.random.normal(ks[0], (B, T, D), dtype=jnp.float32)
        ln_gamma = jnp.ones((D,), dtype=jnp.float32)
        ln_beta = jnp.zeros((D,), dtype=jnp.float32)
        s = 1.0 / np.sqrt(D)
        W_qkv = jax.random.uniform(ks[1], (D, 3 * D), minval=-s, maxval=s, dtype=jnp.float32)
        b_qkv = jax.random.uniform(ks[2], (3 * D,), minval=-s, maxval=s, dtype=jnp.float32)
        W_proj = jax.random.uniform(ks[3], (D, D), minval=-s, maxval=s, dtype=jnp.float32)
        b_proj = jax.random.uniform(ks[4], (D,), minval=-s, maxval=s, dtype=jnp.float32)
        return {'x': x, 'ln_gamma': ln_gamma, 'ln_beta': ln_beta, 'W_qkv': W_qkv, 'b_qkv': b_qkv, 'W_proj': W_proj, 'b_proj': b_proj}
    _L0_attn_all = _L0_attn_setup()
    _L0_attn_in = {k: v for k, v in _L0_attn_all.items() if k in ('ln_gamma', 'ln_beta', 'W_qkv', 'b_qkv', 'W_proj', 'b_proj')}
    del _L0_attn_all

    def _L0_ffn_setup():
        import jax, jax.numpy as jnp
        import numpy as np
        E = 8
        K = 2
        D = 256
        H = 256
        B, T = (2, 256)
        key = jax.random.key(seed)
        ks = jax.random.split(key, 6)
        s = 0.02
        return {'x': jax.random.normal(ks[0], (B, T, D), dtype=jnp.float32), 'gate_w': jax.random.normal(ks[1], (E, D), dtype=jnp.float32) * s, 'lb_bias': jnp.zeros((E,), dtype=jnp.float32), 'w1': jax.random.normal(ks[2], (E, H, D), dtype=jnp.float32) * s, 'w2': jax.random.normal(ks[3], (E, D, H), dtype=jnp.float32) * s, 'cfc': jax.random.normal(ks[4], (H, D), dtype=jnp.float32) * s, 'cproj': jax.random.normal(ks[5], (D, H), dtype=jnp.float32) * s}
    _L0_ffn_all = _L0_ffn_setup()
    _L0_ffn_in = {k: v for k, v in _L0_ffn_all.items() if k in ('gate_w', 'lb_bias', 'w1', 'w2', 'cfc', 'cproj')}
    del _L0_ffn_all

    def _L1_attn_setup():
        import math
        import jax, jax.numpy as jnp
        import numpy as np
        HIDDEN = 256
        HEADS = 16
        HEAD_DIM = HIDDEN // HEADS
        KERNEL = 7
        DILATION = 1
        SCALE = 1.0 / math.sqrt(HEAD_DIM)
        BATCH, SEQ = (2, 512)

        def neighborhood_mask(seq_len: int) -> jnp.ndarray:
            half = KERNEL // 2
            i = jnp.arange(seq_len)[:, None]
            j = jnp.arange(seq_len)[None, :]
            d = j - i
            return (jnp.abs(d) <= half * DILATION) & (d % DILATION == 0)
        key = jax.random.key(seed)
        ks = jax.random.split(key, 9)
        s = 0.02
        return {'hidden_states': jax.random.normal(ks[0], (BATCH, SEQ, HIDDEN), jnp.float32), 'Wq': jax.random.normal(ks[1], (HIDDEN, HIDDEN), jnp.float32) * s, 'bq': jnp.zeros((HIDDEN,), jnp.float32), 'Wk': jax.random.normal(ks[2], (HIDDEN, HIDDEN), jnp.float32) * s, 'bk': jnp.zeros((HIDDEN,), jnp.float32), 'Wv': jax.random.normal(ks[3], (HIDDEN, HIDDEN), jnp.float32) * s, 'bv': jnp.zeros((HIDDEN,), jnp.float32), 'Wo': jax.random.normal(ks[4], (HIDDEN, HIDDEN), jnp.float32) * s, 'bo': jnp.zeros((HIDDEN,), jnp.float32)}
    _L1_attn_all = _L1_attn_setup()
    _L1_attn_in = {k: v for k, v in _L1_attn_all.items() if k in ('Wq', 'bq', 'Wk', 'bk', 'Wv', 'bv', 'Wo', 'bo')}
    del _L1_attn_all

    def _L1_ffn_setup():
        import jax, jax.numpy as jnp
        import numpy as np
        CAPACITY_FACTOR = 1.25
        key = jax.random.key(seed)
        k1, k2, k3, k4 = jax.random.split(key, 4)
        B, T, D, F, E = (4, 1024, 256, 1024, 8)
        s = 0.02
        return {'x': jax.random.normal(k1, (B, T, D), dtype=jnp.float32), 'wg': jax.random.normal(k2, (D, E), dtype=jnp.float32) * s, 'W1': jax.random.normal(k3, (E, D, F), dtype=jnp.float32) * s, 'b1': jnp.zeros((E, F), dtype=jnp.float32), 'W2': jax.random.normal(k4, (E, F, D), dtype=jnp.float32) * s, 'b2': jnp.zeros((E, D), dtype=jnp.float32)}
    _L1_ffn_all = _L1_ffn_setup()
    _L1_ffn_in = {k: v for k, v in _L1_ffn_all.items() if k in ('wg', 'W1', 'b1', 'W2', 'b2')}
    del _L1_ffn_all
    return {'x': x, 'cls_tok': cls_tok, 'L0_tok_ln1_g': _L0_tok_in['ln1_g'], 'L0_tok_ln1_b': _L0_tok_in['ln1_b'], 'L0_tok_W_proj': _L0_tok_in['W_proj'], 'L0_tok_b_proj': _L0_tok_in['b_proj'], 'L0_tok_ln2_g': _L0_tok_in['ln2_g'], 'L0_tok_ln2_b': _L0_tok_in['ln2_b'], 'L0_tok_cls_token': _L0_tok_in['cls_token'], 'L0_tok_pos_emb': _L0_tok_in['pos_emb'], 'L0_attn_ln_gamma': _L0_attn_in['ln_gamma'], 'L0_attn_ln_beta': _L0_attn_in['ln_beta'], 'L0_attn_W_qkv': _L0_attn_in['W_qkv'], 'L0_attn_b_qkv': _L0_attn_in['b_qkv'], 'L0_attn_W_proj': _L0_attn_in['W_proj'], 'L0_attn_b_proj': _L0_attn_in['b_proj'], 'L0_ffn_gate_w': _L0_ffn_in['gate_w'], 'L0_ffn_lb_bias': _L0_ffn_in['lb_bias'], 'L0_ffn_w1': _L0_ffn_in['w1'], 'L0_ffn_w2': _L0_ffn_in['w2'], 'L0_ffn_cfc': _L0_ffn_in['cfc'], 'L0_ffn_cproj': _L0_ffn_in['cproj'], 'L1_attn_Wq': _L1_attn_in['Wq'], 'L1_attn_bq': _L1_attn_in['bq'], 'L1_attn_Wk': _L1_attn_in['Wk'], 'L1_attn_bk': _L1_attn_in['bk'], 'L1_attn_Wv': _L1_attn_in['Wv'], 'L1_attn_bv': _L1_attn_in['bv'], 'L1_attn_Wo': _L1_attn_in['Wo'], 'L1_attn_bo': _L1_attn_in['bo'], 'L1_ffn_wg': _L1_ffn_in['wg'], 'L1_ffn_W1': _L1_ffn_in['W1'], 'L1_ffn_b1': _L1_ffn_in['b1'], 'L1_ffn_W2': _L1_ffn_in['W2'], 'L1_ffn_b2': _L1_ffn_in['b2']}

def reference(x, cls_tok, L0_tok_ln1_g, L0_tok_ln1_b, L0_tok_W_proj, L0_tok_b_proj, L0_tok_ln2_g, L0_tok_ln2_b, L0_tok_cls_token, L0_tok_pos_emb, L0_attn_ln_gamma, L0_attn_ln_beta, L0_attn_W_qkv, L0_attn_b_qkv, L0_attn_W_proj, L0_attn_b_proj, L0_ffn_gate_w, L0_ffn_lb_bias, L0_ffn_w1, L0_ffn_w2, L0_ffn_cfc, L0_ffn_cproj, L1_attn_Wq, L1_attn_bq, L1_attn_Wk, L1_attn_bk, L1_attn_Wv, L1_attn_bv, L1_attn_Wo, L1_attn_bo, L1_ffn_wg, L1_ffn_W1, L1_ffn_b1, L1_ffn_W2, L1_ffn_b2):
    import jax
    import jax.numpy as jnp

    def _L0_tok_ref(x, ln1_g, ln1_b, W_proj, b_proj, ln2_g, ln2_b, cls_token, pos_emb):
        import jax, jax.numpy as jnp
        import numpy as np
        B, C, H, W = (64, 3, 96, 96)
        P = 16
        NP = H // P * (W // P)
        PD = C * P * P
        ED = 256
        NCLS = 1

        def _layernorm(x, g, b, eps=1e-05):
            mu = jnp.mean(x, axis=-1, keepdims=True)
            var = jnp.mean(jnp.square(x - mu), axis=-1, keepdims=True)
            return (x - mu) * jax.lax.rsqrt(var + eps) * g + b
        b = x.shape[0]
        h, w = (H // P, W // P)
        patches = x.reshape(b, C, h, P, w, P)
        patches = patches.transpose(0, 2, 4, 3, 5, 1).reshape(b, h * w, P * P * C)
        z = _layernorm(patches, ln1_g, ln1_b)
        z = jnp.einsum('bnp,pe->bne', z, W_proj) + b_proj
        z = _layernorm(z, ln2_g, ln2_b)
        cls = jnp.broadcast_to(cls_token, (b, NCLS, ED))
        z = jnp.concatenate([cls, z], axis=1)
        z = z + pos_emb
        return z

    def _L0_attn_ref(x, ln_gamma, ln_beta, W_qkv, b_qkv, W_proj, b_proj):
        import jax, jax.numpy as jnp
        import numpy as np
        D_MODEL = 256
        NHEAD = 16
        HEAD_DIM = D_MODEL // NHEAD
        SCALE = HEAD_DIM ** (-0.5)
        EPS_LN = 1e-05
        B, T, D = x.shape
        h, dh = (NHEAD, HEAD_DIM)
        mu = jnp.mean(x, axis=-1, keepdims=True)
        var = jnp.mean(jnp.square(x - mu), axis=-1, keepdims=True)
        x_n = (x - mu) * jax.lax.rsqrt(var + EPS_LN) * ln_gamma + ln_beta
        qkv = x_n @ W_qkv + b_qkv
        q, k, v = jnp.split(qkv, 3, axis=-1)
        q = q.reshape(B, T, h, dh).transpose(0, 2, 1, 3)
        k = k.reshape(B, T, h, dh).transpose(0, 2, 1, 3)
        v = v.reshape(B, T, h, dh).transpose(0, 2, 1, 3)
        scores = jnp.einsum('bhqd,bhkd->bhqk', q, k) * SCALE
        scores = scores - jnp.max(scores, axis=-1, keepdims=True)
        attn = jnp.exp(scores)
        attn = attn / jnp.maximum(jnp.sum(attn, axis=-1, keepdims=True), 1e-12)
        ctx = jnp.einsum('bhqk,bhkd->bhqd', attn, v)
        ctx = ctx.transpose(0, 2, 1, 3).reshape(B, T, D)
        return ctx @ W_proj + b_proj

    def _L0_ffn_ref(x, gate_w, lb_bias, w1, w2, cfc, cproj):
        import jax, jax.numpy as jnp
        import numpy as np
        E = 8
        K = 2
        D = 256
        H = 256
        B, T = (2, 256)
        Bx, Tx, Dx = x.shape
        logits = jnp.einsum('btd,ed->bte', x, gate_w)
        _, idx = jax.lax.top_k(logits + lb_bias, K)
        sel_logits = jnp.take_along_axis(logits, idx, axis=-1)
        w = jax.nn.sigmoid(sel_logits)
        w = w / (jnp.sum(w, axis=-1, keepdims=True) + 1e-06)
        xf = x.reshape(-1, Dx)
        idxf = idx.reshape(-1, K)
        wf = w.reshape(-1, K)
        onehot = jax.nn.one_hot(idxf, E, dtype=wf.dtype)
        we = jnp.einsum('nke,nk->ne', onehot, wf)
        hidden = jnp.square(jax.nn.relu(jnp.einsum('nd,ehd->neh', xf, w1)))
        expert_out = jnp.einsum('neh,edh->ned', hidden, w2)
        moe_out = jnp.einsum('ned,ne->nd', expert_out, we).reshape(Bx, Tx, Dx)
        sh = jnp.square(jax.nn.relu(jnp.einsum('btd,hd->bth', x, cfc)))
        shared = jnp.einsum('bth,dh->btd', sh, cproj)
        return moe_out + shared

    def _L1_attn_ref(hidden_states, Wq, bq, Wk, bk, Wv, bv, Wo, bo):
        import math
        import jax, jax.numpy as jnp
        import numpy as np
        HIDDEN = 256
        HEADS = 16
        HEAD_DIM = HIDDEN // HEADS
        KERNEL = 7
        DILATION = 1
        SCALE = 1.0 / math.sqrt(HEAD_DIM)
        BATCH, SEQ = (2, 512)

        def neighborhood_mask(seq_len: int) -> jnp.ndarray:
            half = KERNEL // 2
            i = jnp.arange(seq_len)[:, None]
            j = jnp.arange(seq_len)[None, :]
            d = j - i
            return (jnp.abs(d) <= half * DILATION) & (d % DILATION == 0)
        B, S, H = hidden_states.shape
        q = hidden_states @ Wq.T + bq
        k = hidden_states @ Wk.T + bk
        v = hidden_states @ Wv.T + bv
        q = q.reshape(B, S, HEADS, HEAD_DIM).transpose(0, 2, 1, 3)
        k = k.reshape(B, S, HEADS, HEAD_DIM).transpose(0, 2, 1, 3)
        v = v.reshape(B, S, HEADS, HEAD_DIM).transpose(0, 2, 1, 3)
        scores = jnp.einsum('bhqd,bhkd->bhqk', q, k) * SCALE
        mask = neighborhood_mask(S)
        scores = jnp.where(mask[None, None], scores, -jnp.inf)
        attn = jax.nn.softmax(scores, axis=-1)
        out = jnp.einsum('bhqk,bhkd->bhqd', attn, v)
        out = out.transpose(0, 2, 1, 3).reshape(B, S, H)
        return out @ Wo.T + bo

    def _L1_ffn_ref(x, wg, W1, b1, W2, b2):
        import jax, jax.numpy as jnp
        import numpy as np
        CAPACITY_FACTOR = 1.25
        B, T, D = x.shape
        E = wg.shape[1]
        N = B * T
        capacity = int(N / E * CAPACITY_FACTOR) + 1
        xf = x.reshape(N, D)
        logits = xf @ wg
        scores = jax.nn.softmax(logits, axis=-1)
        top1 = jnp.argmax(scores, axis=-1)
        combine_w = jnp.take_along_axis(scores, top1[:, None], axis=1)[:, 0]
        oh = jax.nn.one_hot(top1, E, dtype=jnp.int32)
        rank = jnp.take_along_axis(jnp.cumsum(oh, axis=0), top1[:, None], axis=1)[:, 0] - 1
        valid = rank < capacity
        trash = E * capacity
        slot = jnp.where(valid, top1 * capacity + rank, trash)
        buf = jnp.zeros((E * capacity + 1, D), dtype=x.dtype).at[slot].set(xf)
        eb = buf[:E * capacity].reshape(E, capacity, D)
        h = jax.nn.gelu(jnp.einsum('ecd,edf->ecf', eb, W1) + b1[:, None, :], approximate=False)
        y = jnp.einsum('ecf,efd->ecd', h, W2) + b2[:, None, :]
        yf = y.reshape(E * capacity, D)
        gathered = yf[jnp.minimum(slot, E * capacity - 1)]
        out_flat = jnp.where(valid[:, None], gathered, 0.0) * combine_w[:, None]
        return out_flat.reshape(B, T, D)
    h = _L0_tok_ref(x, L0_tok_ln1_g, L0_tok_ln1_b, L0_tok_W_proj, L0_tok_b_proj, L0_tok_ln2_g, L0_tok_ln2_b, L0_tok_cls_token, L0_tok_pos_emb)
    h = jnp.concatenate([jnp.broadcast_to(cls_tok, (h.shape[0], 1, h.shape[2])), h], axis=1)
    h = h + _L0_attn_ref(_layernorm(h, axis=-1), L0_attn_ln_gamma, L0_attn_ln_beta, L0_attn_W_qkv, L0_attn_b_qkv, L0_attn_W_proj, L0_attn_b_proj)
    h = h + _L0_ffn_ref(_layernorm(h, axis=-1), L0_ffn_gate_w, L0_ffn_lb_bias, L0_ffn_w1, L0_ffn_w2, L0_ffn_cfc, L0_ffn_cproj)
    h = h + _L1_attn_ref(_layernorm(h, axis=-1), L1_attn_Wq, L1_attn_bq, L1_attn_Wk, L1_attn_bk, L1_attn_Wv, L1_attn_bv, L1_attn_Wo, L1_attn_bo)
    h = h + _L1_ffn_ref(_layernorm(h, axis=-1), L1_ffn_wg, L1_ffn_W1, L1_ffn_b1, L1_ffn_W2, L1_ffn_b2)
    return h

_drawn_inputs = setup_inputs


def setup_inputs(seed=0):
    import zlib

    import numpy as np

    out = dict(_drawn_inputs(seed))
    spreads = {'L0_tok_ln1_g': (1.0, 0.2),
     'L0_tok_ln1_b': (0.0, 0.1),
     'L0_tok_b_proj': (0.0, 0.1),
     'L0_tok_ln2_g': (1.0, 0.2),
     'L0_tok_ln2_b': (0.0, 0.1),
     'L0_attn_ln_gamma': (1.0, 0.6),
     'L0_attn_ln_beta': (0.0, 0.277),
     'L0_ffn_lb_bias': (0.0, 0.738),
     'L1_attn_bq': (0.0, 0.8),
     'L1_attn_bk': (0.0, 0.8),
     'L1_attn_bv': (0.0, 0.36),
     'L1_attn_bo': (0.0, 0.1),
     'L1_ffn_b1': (0.0, 0.8),
     'L1_ffn_b2': (0.0, 0.614)}
    factors = {'cls_tok': 6.722,
     'L0_attn_b_qkv': 3.104,
     'L0_ffn_gate_w': 2.765,
     'L0_ffn_w1': 3.126,
     'L0_ffn_w2': 2.84,
     'L1_attn_Wq': 8.0,
     'L1_attn_Wk': 8.0,
     'L1_ffn_wg': 3.105,
     'L1_ffn_W1': 4.096,
     'L1_ffn_W2': 3.815}
    for name, (base, spread) in spreads.items():
        noise = np.random.default_rng([zlib.crc32(name.encode()), seed]).standard_normal(out[name].shape)
        drawn = base * np.exp(spread * noise) if base else spread * noise
        out[name] = jnp.asarray(drawn.astype(out[name].dtype))
    for name, factor in factors.items():
        out[name] = (out[name] * factor).astype(out[name].dtype)
    return out
```

```python
import concourse.bass as bass
from concourse import mybir
from contextlib import ExitStack

ALU = mybir.AluOpType
ACT = mybir.ActivationFunctionType
AX_X = mybir.AxisListType.X
F32 = mybir.dt.float32
BF16 = mybir.dt.bfloat16
U32 = mybir.dt.uint32

P = 128
B = 16
T = 38
N = B * T
NT = 5
NP = NT * P
HALF = N // 2
D = 256
KC = D // P
PD = 768
PC = PD // P
H = 16
DH = D // H
HM = P // DH
NPAIR = B // 2
SLOT = 64
E = 8
CAP = int(N / E * 1.25) + 1
FF = 1024
FC = FF // P
SCALE = float(DH) ** -0.5
EPS = 1e-5
TOK_GROUPS = ((0, 3), (3, 5))
RING = 3

COLS = {}
_at = 0
for _name, _n in (("ln1_g", PC), ("ln1_b", PC), ("lng", KC), ("lnb", KC),
                  ("bq0", KC), ("bk0", KC), ("bv0", KC), ("bq1", KC), ("bk1", KC), ("bv1", KC),
                  ("b1", E * FC), ("head", HM), ("slot0", E)):
    COLS[_name] = (_at, _at + _n)
    _at += _n
NCOLS = _at
ROWS = {}
_at = 0
for _name, _n in (("bz", D), ("bo0", D), ("bo1", D), ("lb", E), ("iota", E)):
    ROWS[_name] = (_at, _at + _n)
    _at += _n
NROWS = _at


def vit_kernel(nc, patches, scale_tok, shift_a, shift_b, w_patch, w_qkv, w_out, gate, w_moe, w_attn1, wg, w1, w2,
               cols, rows, b2_rows, iota_slots, ident, band, spread, upper, out):
    with ExitStack() as ctx:
        def sb(name, shape, dt=F32):
            return ctx.enter_context(nc.sbuf_tensor(name, shape, dt))

        def sem(name):
            return ctx.enter_context(nc.semaphore(name))

        def part(whole, at, shape, dt=F32):
            n = 1
            for x in shape:
                n *= x
            words = n // 2 if dt == BF16 else n
            ap = whole[:, at:at + words]
            if dt == BF16:
                ap = ap.bitcast(BF16)
            names = "abcd"[:len(shape)]
            spec = f"p ({' '.join(names)}) -> p {' '.join(names)}"
            return ap.rearrange(spec, **dict(zip(names, shape))), at + words

        ps = ctx.enter_context(nc.psum_tensor("ps", [P, 8, 512], F32))

        col = sb("col", [P, NCOLS])
        row = sb("row", [P, NROWS])
        idn = sb("idn", [P, P])
        bandm = sb("bandm", [T, HM * T], BF16)
        spreadm = sb("spreadm", [T, P], BF16)
        upperm = sb("upperm", [P, 2, P], BF16)
        onesm = sb("onesm", [P, P])
        neghalf = sb("neghalf", [P, NT])
        wo0 = sb("wo0", [P, KC, D])
        gatew = sb("gatew", [P, KC, E])
        wgw = sb("wgw", [P, KC, E])
        wat1 = sb("wat1", [P, KC, 4 * D])
        weights = sb("weights", [P, RING * (KC * FF + FC * D)])
        wmoe, _ = part(weights, 0, [E + 1, 2 * KC, D])
        fw1, at = part(weights, 0, [RING, KC, FF])
        fw2, at = part(weights, at, [RING, FC, D])
        early = sb("early", [P, PC * D + KC * 3 * D])
        wz, at = part(early, 0, [PC, D])
        wqkv0, _ = part(early, at, [KC, 3 * D])
        b2r, at = part(early, 0, [E, D])
        iota, _ = part(early, at, [E * CAP])
        work = sb("work", [P, NT * PD + PC * NP + 3 * NT * D])
        tok, at = part(work, 0, [NT, PD])
        ztr, at = part(work, at, [PC, NP])
        gsc, at = part(work, at, [NT, D])
        sha, at = part(work, at, [NT, D])
        shb, at = part(work, at, [NT, D])
        kbd, _ = part(work, 0, [KC, HM, N])
        rl, at = part(work, 0, [2, 2, HALF])
        hid, _ = part(work, at, [2, KC, N])
        x3, at = part(work, 0, [3, NT, D], BF16)
        sel, at = part(work, at, [NT, E * CAP], BF16)
        selT, at = part(work, at, [E, NP])
        ye, at = part(work, at, [E, D])
        values = sb("values", [P, B * HM * 2 * DH])
        vbd, _ = part(values, 0, [B, HM, 2 * DH])
        xg, at = part(values, 0, [KC, E * CAP])
        hT, at = part(values, at, [2, FC, CAP])
        dg, at = part(values, at, [NT, P])
        zt = sb("zt", [P, NT, D])
        h = sb("h", [P, NT, D])
        hb = sb("hb", [P, NT, D])
        xn = sb("xn", [P, NT, D])
        xT = sb("xT", [P, KC, NP])
        qT = sb("qT", [P, KC, NP])
        kT = sb("kT", [P, KC, N])
        oT = sb("oT", [P, KC, NP])
        st = sb("st", [P, NT, 2, 6])
        mv = sb("mv", [P, NT, 2])
        ve = sb("ve", [P, NT])
        rstd = sb("rstd", [P, NT])
        sd = sb("sd", [P, 2, H, T])
        pe_ = sb("pe_", [P, 3, H, SLOT])
        mx = sb("mx", [P, 2, H])
        rs = sb("rs", [P, 3, H])
        ri = sb("ri", [P, 3, H])
        pT = sb("pT", [P, 2, HM, 2, T])
        lg = sb("lg", [P, NT, E])
        lgb = sb("lgb", [P, NT, E])
        m8 = sb("m8", [P, NT, 8])
        i8 = sb("i8", [P, NT, 8], U32)
        i8f = sb("i8f", [P, NT, 2])
        ga = sb("ga", [P, NT, E])
        gb = sb("gb", [P, NT, E])
        sg = sb("sg", [P, NT, E])
        we = sb("we", [P, NT, E])
        s5 = sb("s5", [P, 4, NT])
        ohb = sb("ohb", [P, NT, E], BF16)
        slotb = sb("slotb", [CAP, NP])
        xr = zt
        res = zt

        def c_(name, i=0, n=1):
            return col[:, COLS[name][0] + i:COLS[name][0] + i + n]

        def r_(name):
            return row[:, ROWS[name][0]:ROWS[name][1]]

        ld_tok = [sem(f"ld_tok{t}") for t in range(NT)]
        ld = {n: sem("ld_" + n) for n in ("col", "row", "b2", "iota", "idn", "masks", "wz", "tokc", "wqkv0", "wo0",
                                          "gate", "wat1")}
        ld_moe = [sem(f"ld_moe{e}") for e in range(E + 1)]
        ld_f = [sem(f"ld_f{r}") for r in range(RING)]
        consts = sem("consts")
        dve = sem("dve")
        pool = sem("pool")
        act = sem("act")
        var_ready = sem("var_ready")
        rstd_ready = sem("rstd_ready")
        pn_ready = sem("pn_ready")
        ztr_ps = sem("ztr_ps")
        ztr_act = sem("ztr_act")
        ztr_dve = sem("ztr_dve")
        z_ps = sem("z_ps")
        shift_ready = sem("shift_ready")
        h_ready = sem("h_ready")
        hb_ready = sem("hb_ready")
        xn_ready = sem("xn_ready")
        xT_ps = sem("xT_ps")
        xT_ready = sem("xT_ready")
        qk_ps = sem("qk_ps")
        kT_ready = sem("kT_ready")
        qT_ready = sem("qT_ready")
        kbd_dve = sem("kbd_dve")
        kbd_pool = sem("kbd_pool")
        v_ps = sem("v_ps")
        vbd_ready = sem("vbd_ready")
        s_ps = sem("s_ps")
        s_shifted = sem("s_shifted")
        exp_ready = sem("exp_ready")
        rs_ready = sem("rs_ready")
        pn = sem("pn")
        pT_ps = sem("pT_ps")
        pT_ready = sem("pT_ready")
        o_ps = sem("o_ps")
        oT_ready = sem("oT_ready")
        proj_ps = sem("proj_ps")
        lg_ps = sem("lg_ps")
        lg_ready = sem("lg_ready")
        ex_ready = sem("ex_ready")
        we_ready = sem("we_ready")
        hid_ps = sem("hid_ps")
        relu_ready = sem("relu_ready")
        hid_ready = sem("hid_ready")
        y_ps = sem("y_ps")
        y_used = sem("y_used")
        x3_act = sem("x3_act")
        x3_dve = sem("x3_dve")
        oh_ready = sem("oh_ready")
        cum_ps = sem("cum_ps")
        dg_ready = sem("dg_ready")
        slotb_ps = sem("slotb_ps")
        slotb_ready = sem("slotb_ready")
        sel_ready = sem("sel_ready")
        selT_ready = sem("selT_ready")
        xg_ps = sem("xg_ps")
        xg_ready = sem("xg_ready")
        fh_ps = sem("fh_ps")
        gelu_ready = sem("gelu_ready")
        fy_ps = sem("fy_ps")
        ye_ready = sem("ye_ready")
        comb_ps = sem("comb_ps")
        res_ready = sem("res_ready")
        stored = sem("stored")

        block = ctx.enter_context(nc.Block())

        @block.sync
        def _(sp):
            def load(dst, src, s):
                sp.dma_start(dst, src).then_inc(s, 16)

            load(tok[:, 0, :], patches[:, 0, :], ld_tok[0])
            load(col[:], cols, ld["col"])
            load(idn[:], ident, ld["idn"])
            for t in range(1, NT):
                load(tok[:, t, :], patches[:, t, :], ld_tok[t])
            load(wz[:], w_patch, ld["wz"])
            load(row[:], rows, ld["row"])
            load(gsc[:], scale_tok, ld["tokc"])
            load(sha[:], shift_a, ld["tokc"])
            load(shb[:], shift_b, ld["tokc"])
            load(wqkv0[:], w_qkv, ld["wqkv0"])
            load(bandm[:], band, ld["masks"])
            load(spreadm[:], spread, ld["masks"])
            load(upperm[:], upper, ld["masks"])
            load(wo0[:], w_out, ld["wo0"])
            load(gatew[:], gate, ld["gate"])
            load(wgw[:], wg, ld["gate"])
            for e in (E, *range(E)):
                load(wmoe[:, e], w_moe[:, e], ld_moe[e])
            load(wat1[:], w_attn1, ld["wat1"])
            sp.wait_ge(y_ps, 3 * (E + 1))
            load(iota[:], iota_slots, ld["iota"])
            load(b2r[:], b2_rows, ld["b2"])
            for e in range(E):
                if e >= RING:
                    sp.wait_ge(fy_ps, e - RING + 1)
                load(fw1[:, e % RING], w1[:, e], ld_f[e % RING])
                load(fw2[:, e % RING], w2[:, e], ld_f[e % RING])
            for t in range(NT):
                n = min(P, N - t * P)
                sp.wait_ge(res_ready, t + 1)
                sp.dma_start(out[t * P:t * P + n, :], res[0:n, t, :]).then_inc(stored, 16)
            sp.wait_ge(stored, 16 * NT)

        @block.gpsimd
        def _(gp):
            own = [0]

            def done(ins):
                own[0] += 1
                ins.then_inc(pool, 1)
                gp.wait_ge(pool, own[0])

            gp.memset(neghalf[:], -0.5).then_inc(consts, 1)
            gp.memset(qT[:, :, N:NP], 0.0).then_inc(consts, 1)
            gp.memset(oT[:, :, N:NP], 0.0).then_inc(consts, 1)
            gp.memset(vbd[:], 0.0).then_inc(consts, 1)
            gp.memset(pe_[:], 0.0).then_inc(consts, 1)
            gp.memset(onesm[:], 1.0).then_inc(consts, 1)
            gp.wait_ge(consts, 6)

            n_rstd = [0]

            def rstd_step(a, b):
                n_rstd[0] += 1
                gp.wait_ge(var_ready, n_rstd[0])
                gp.tensor_tensor(rstd[:, a:b], ve[:, a:b], neghalf[:, a:b], ALU.pow).then_inc(rstd_ready, 1)

            for t in range(NT):
                rstd_step(t, t + 1)
            gp.wait_ge(ld["tokc"], 48)
            gp.tensor_tensor(shb[:], sha[:], shb[:], ALU.add).then_inc(shift_ready, 1)
            rstd_step(0, NT)

            def add_bias(name, n):
                gp.wait_ge(h_ready, n)
                for t in range(NT):
                    ins = gp.tensor_tensor(hb[:, t, :], h[:, t, :], r_(name), ALU.add)
                ins.then_inc(hb_ready, 1)

            def attention(layer):
                for m in range(KC):
                    gp.wait_ge(kT_ready, 4 * layer + 2 * m + 2)
                    for hh in range(HM // 2, HM):
                        ins = gp.tensor_scalar(kbd[:, m, hh, :], kT[:, m, :], c_("head", hh), 1.0, ALU.mult, ALU.mult)
                    ins.then_inc(kbd_pool, 1)
                for p in range(NPAIR):
                    gp.wait_ge(rs_ready, layer * NPAIR + p + 1)
                    w = pe_[:, p % 3, :, 0:T]
                    gp.tensor_tensor(w, w, ri[:, p % 3, :].unsqueeze(2).broadcast_to([P, H, T]), ALU.mult)\
                      .then_inc(pn, 1)

            add_bias("bo0", 1)
            rstd_step(0, NT)
            rstd_step(0, NT)
            attention(0)
            rstd_step(0, NT)
            rstd_step(0, NT)
            add_bias("bo1", 3)
            attention(1)
            rstd_step(0, NT)

        @block.scalar
        def _(sc):
            for g, (a, b) in enumerate(TOK_GROUPS):
                for c in range(0, PC, 2):
                    j = g * PC + c
                    if j == 0:
                        sc.wait_ge(ld["col"], 16)
                    sc.wait_ge(ztr_ps, j + 1)
                    sc.activation(ztr[:, c, a * P:b * P], ps[:, j % 4, 0:(b - a) * P], ACT.Identity,
                                  scale=c_("ln1_g", c), bias=c_("ln1_b", c)).then_inc(ztr_act, 1)

            n_xT = [0]

            def xT_evict(first):
                for g, (a, b) in enumerate(TOK_GROUPS):
                    for c in range(KC):
                        n_xT[0] += 1
                        j = 2 * g + c
                        sc.wait_ge(xT_ps, n_xT[0])
                        if first:
                            sc.activation(xT[:, c, a * P:b * P], ps[:, j, 0:(b - a) * P], ACT.Identity,
                                          scale=c_("lng", c), bias=c_("lnb", c)).then_inc(xT_ready, 1)
                        else:
                            sc.copy(xT[:, c, a * P:b * P], ps[:, j, 0:(b - a) * P]).then_inc(xT_ready, 1)

            def attention(layer):
                xT_evict(layer == 0)
                for i, (dst, name, ready) in enumerate(((kT, "bk", kT_ready), (qT, "bq", qT_ready))):
                    for m in range(KC):
                        for half in range(2):
                            n = 4 * i + 2 * m + half
                            sc.wait_ge(qk_ps, 8 * layer + n + 1)
                            sc.activation(dst[:, m, half * HALF:(half + 1) * HALF], ps[:, n, 0:HALF],
                                          ACT.Identity, bias=c_(f"{name}{layer}", m)).then_inc(ready, 1)
                for g in range(4):
                    sc.wait_ge(v_ps, 4 * layer + g + 1)
                    for par in range(2):
                        q = slice(par * SLOT, (par + 1) * SLOT)
                        src = ps[q, g, :].rearrange("p (b h d) -> p b h d", b=4, h=HM)
                        sc.copy(vbd[q, 4 * g:4 * g + 4, :, par * DH:(par + 1) * DH], src).then_inc(vbd_ready, 1)
                for i in range(NPAIR + 2):
                    if i < NPAIR:
                        n = layer * NPAIR + i
                        sc.wait_ge(s_shifted, n + 1)
                        if i >= 3:
                            sc.wait_ge(pT_ps, n - 3 + 1)
                        sc.activation(pe_[:, i % 3, :, 0:T], sd[:, i % 2], ACT.Exp, scale=SCALE)\
                          .then_inc(exp_ready, 1)
                    if i >= 2:
                        n = layer * NPAIR + i - 2
                        sc.wait_ge(pT_ps, n + 1)
                        if i - 2 >= 2:
                            sc.wait_ge(o_ps, n - 2 + 1)
                        src = ps[:, 0:2, :].rearrange("p k (h b s) -> p (k h) b s", h=4, b=2)
                        sc.copy(pT[:, i % 2], src[:, :, :, 0:T]).then_inc(pT_ready, 1)

            attention(0)
            xT_evict(False)
            sc.wait_ge(lg_ready, 1)
            sc.activation(sg[:], lg[:], ACT.Exp, scale=-1.0).then_inc(ex_ready, 1)
            for i in range(2 * (E + 1)):
                sc.wait_ge(hid_ps, i + 1)
                if i >= 2:
                    sc.wait_ge(hid_ready, i - 1)
                m = i % 2
                sc.activation(rl[:, m], ps[:, 2 * m:2 * m + 2, 0:HALF], ACT.Relu).then_inc(relu_ready, 1)
            attention(1)
            xT_evict(False)
            sc.wait_ge(xn_ready, 4 * NT)
            sc.copy(x3[:, 0], xn[:]).then_inc(x3_act, 1)
            sc.wait_ge(x3_dve, 1)
            sc.copy(x3[:, 1], xr[:]).then_inc(x3_act, 1)
            sc.wait_ge(x3_dve, 2)
            sc.copy(x3[:, 2], xr[:]).then_inc(x3_act, 1)
            sc.wait_ge(lg_ready, 2)
            sc.activation(sg[:], ga[:], ACT.Exp).then_inc(ex_ready, 1)
            for i, (a, b) in enumerate(((0, 512), (512, NP))):
                sc.wait_ge(slotb_ps, i + 1)
                sc.copy(slotb[:, a:b], ps[0:CAP, 6 + i, 0:b - a]).then_inc(slotb_ready, 1)
            half_slots = E * CAP // 2
            for j in range(4):
                sc.wait_ge(xg_ps, j + 1)
                s = j // 2
                sc.copy(xg[:, j % 2, s * half_slots:(s + 1) * half_slots], ps[:, j, 0:half_slots])\
                  .then_inc(xg_ready, 1)
            for e in range(E):
                for q in range(2):
                    sc.wait_ge(fh_ps, 2 * e + q + 1)
                    if e >= 2 and q == 0:
                        sc.wait_ge(fy_ps, e - 1)
                    for f in range(4 * q, 4 * q + 4):
                        ins = sc.activation(hT[:, e % 2, f, :], ps[:, 2 * (e % 2) + q, (f % 4) * CAP:(f % 4 + 1) * CAP],
                                            ACT.Gelu, bias=c_("b1", e * FC + f))
                    ins.then_inc(gelu_ready, 1)

        @block.vector
        def _(v):
            own = [0]

            def done(ins):
                own[0] += 1
                ins.then_inc(dve, 1)
                v.wait_ge(dve, own[0])

            def mark(ins):
                own[0] += 1
                ins.then_inc(dve, 1)

            def sync_own():
                v.wait_ge(dve, own[0])

            n_rstd = [0]

            def patch_stats(t):
                v.wait_ge(ld_tok[t], 16)
                for k in range(2):
                    ins = v.bn_stats(st[:, t, k, :], tok[:, t, k * (PD // 2):(k + 1) * (PD // 2)])
                    mark(ins)
                sync_own()
                done(v.bn_aggr(mv[:, t, :], st[:, t].rearrange("p k s -> p (k s)")))
                v.tensor_scalar(ve[:, t:t + 1], mv[:, t, 1:2], EPS, None, ALU.add).then_inc(var_ready, 1)

            def patch_norm(t):
                n_rstd[0] += 1
                v.wait_ge(rstd_ready, n_rstd[0])
                v.tensor_scalar(tok[:, t, :], tok[:, t, :], mv[:, t, 0:1], rstd[:, t:t + 1],
                                ALU.subtract, ALU.mult).then_inc(pn_ready, 1)

            def patch_evict(g):
                a, b = TOK_GROUPS[g]
                for c in range(1, PC, 2):
                    j = g * PC + c
                    v.wait_ge(ztr_ps, j + 1)
                    v.tensor_scalar(ztr[:, c, a * P:b * P], ps[:, j % 4, 0:(b - a) * P], c_("ln1_g", c),
                                    c_("ln1_b", c), ALU.mult, ALU.add).then_inc(ztr_dve, 1)

            def stats(src, t):
                done(v.bn_stats(st[:, t, 0, :], src[:, t, :]))
                mark(v.bn_aggr(mv[:, t, :], st[:, t, 0, :]))

            def norm(dst, src, ready):
                sync_own()
                v.tensor_scalar(ve[:], mv[:, :, 1], EPS, None, ALU.add).then_inc(var_ready, 1)
                n_rstd[0] += 1
                v.wait_ge(rstd_ready, n_rstd[0])
                for t in range(NT):
                    ins = v.tensor_scalar(dst[:, t, :], src[:, t, :], mv[:, t, 0:1], rstd[:, t:t + 1],
                                          ALU.subtract, ALU.mult)
                    if ready is None:
                        mark(ins)
                    else:
                        ins.then_inc(ready, 1)

            patch_stats(0)
            for t in range(1, NT):
                patch_stats(t)
                patch_norm(t - 1)
                if t == 3:
                    v.wait_ge(ld["col"], 16)
                    patch_evict(0)
            patch_norm(NT - 1)
            patch_evict(1)
            v.wait_ge(ld["row"], 16)
            for t in range(NT):
                v.wait_ge(z_ps, t + 1)
                done(v.tensor_tensor(zt[:, t, :], ps[:, (4 + t) % 8, 0:D], r_("bz"), ALU.add))
                stats(zt, t)
            norm(zt, zt, None)
            v.wait_ge(ld["tokc"], 48)
            sync_own()
            done(v.tensor_tensor(zt[:], zt[:], gsc[:], ALU.mult))
            v.wait_ge(shift_ready, 1)
            v.tensor_tensor(h[:], zt[:], shb[:], ALU.add).then_inc(h_ready, 1)
            v.wait_ge(h_ready, 1)

            def attention(layer):
                for m in range(KC):
                    v.wait_ge(kT_ready, 4 * layer + 2 * m + 2)
                    for hh in range(HM // 2):
                        ins = v.tensor_scalar(kbd[:, m, hh, :], kT[:, m, :], c_("head", hh), None, ALU.mult)
                    ins.then_inc(kbd_dve, 1)
                for i in range(NPAIR + 3):
                    if i < NPAIR:
                        n = layer * NPAIR + i
                        v.wait_ge(s_ps, n + 1)
                        s = ps[:, 4 + 2 * (i % 2):6 + 2 * (i % 2), 0:HM * T].rearrange("p m (h k) -> p m h k", h=HM)
                        done(v.tensor_reduce(mx[:, i % 2, :].rearrange("p (m h) -> p m h", m=KC), s, AX_X, ALU.max))
                        if i >= 2:
                            v.wait_ge(exp_ready, n - 1)
                        mb = mx[:, i % 2, :].rearrange("p (m h) -> p m h", m=KC).unsqueeze(3)
                        v.tensor_tensor(sd[:, i % 2].rearrange("p (m h) k -> p m h k", m=KC), s,
                                        mb.broadcast_to([P, KC, HM, T]), ALU.subtract).then_inc(s_shifted, 1)
                    if 1 <= i <= NPAIR:
                        r = (i - 1) % 3
                        v.wait_ge(exp_ready, layer * NPAIR + i)
                        done(v.tensor_reduce(rs[:, r, :], pe_[:, r, :, 0:T], AX_X, ALU.add))
                        v.reciprocal(ri[:, r, :], rs[:, r, :]).then_inc(rs_ready, 1)
                    if i >= 3:
                        p = i - 3
                        v.wait_ge(o_ps, layer * NPAIR + p + 1)
                        a, b = COLS[f"bv{layer}"]
                        v.tensor_tensor(oT[:, :, p * 2 * T:(p + 1) * 2 * T],
                                        ps[:, 2 + p % 2, 0:KC * 2 * T].rearrange("p (m n) -> p m n", m=KC),
                                        col[:, a:b].unsqueeze(2).broadcast_to([P, KC, 2 * T]), ALU.add)\
                         .then_inc(oT_ready, 1)
                for t in range(NT):
                    v.wait_ge(proj_ps, layer * NT + t + 1)
                    if t == 0:
                        v.wait_ge(hb_ready, layer + 1)
                    done(v.tensor_tensor(h[:, t, :], ps[:, (4 + t) % 8, 0:D], hb[:, t, :], ALU.add))
                    stats(h, t)

            for t in range(NT):
                stats(h, t)
            norm(xn, h, None)
            sync_own()
            for t in range(NT):
                stats(xn, t)
            norm(xn, xn, xn_ready)
            attention(0)

            norm(xn, h, xn_ready)
            v.wait_ge(lg_ps, 1)
            v.tensor_copy(lg[:], ps[:, 4, 0:NT * E].rearrange("p (t e) -> p t e", e=E)).then_inc(lg_ready, 1)
            v.wait_ge(lg_ready, 1)
            done(v.tensor_tensor(lgb[:], lg[:], r_("lb").unsqueeze(1).broadcast_to([P, NT, E]), ALU.add))
            for t in range(NT):
                done(v.max(m8[:, t, :], lgb[:, t, :]))
                mark(v.max_index(i8[:, t, :], m8[:, t, :], lgb[:, t, :]))
            sync_own()
            done(v.tensor_copy(i8f[:], i8[:, :, 0:2]))
            bc = [P, NT, E]
            it = r_("iota").unsqueeze(1).broadcast_to(bc)
            mark(v.tensor_tensor(ga[:], it, i8f[:, :, 0:1].broadcast_to(bc), ALU.is_equal))
            done(v.tensor_tensor(gb[:], it, i8f[:, :, 1:2].broadcast_to(bc), ALU.is_equal))
            done(v.tensor_tensor(ga[:], ga[:], gb[:], ALU.add))
            v.wait_ge(ex_ready, 1)
            done(v.tensor_scalar(gb[:], sg[:], 1.0, None, ALU.add))
            done(v.reciprocal(sg[:], gb[:]))
            done(v.tensor_tensor(gb[:], sg[:], ga[:], ALU.mult))
            done(v.tensor_reduce(s5[:, 0, :], gb[:], AX_X, ALU.add))
            done(v.tensor_scalar(s5[:, 1, :], s5[:, 0, :], 1e-6, None, ALU.add))
            done(v.reciprocal(s5[:, 2, :], s5[:, 1, :]))
            done(v.tensor_tensor(we[:], gb[:], s5[:, 2, :].unsqueeze(2).broadcast_to(bc), ALU.mult))

            def squares(n):
                for m in range(KC):
                    v.wait_ge(relu_ready, 2 * n + m + 1)
                    if n >= 2 and m == 0:
                        v.wait_ge(y_ps, 3 * (n - 1))
                    v.tensor_tensor(hid[:, n % 2, m, :].rearrange("p (a b) -> p a b", a=2), rl[:, m], rl[:, m],
                                    ALU.mult).then_inc(hid_ready, 1)

            def add_expert(n):
                for k, tiles in enumerate(((0, 1), (2, 3), (4,))):
                    v.wait_ge(y_ps, 3 * n + k + 1)
                    for t in tiles:
                        m = min(P, N - t * P)
                        y = ps[0:m, 5 + k, (t % 2) * D:(t % 2 + 1) * D]
                        if n == 0:
                            ins = v.tensor_tensor(h[0:m, t, :], y, h[0:m, t, :], ALU.add)
                        else:
                            ins = v.scalar_tensor_tensor(out=h[0:m, t, :], in0=y, scalar=we[0:m, t, n - 1:n],
                                                         in1=h[0:m, t, :], op0=ALU.mult, op1=ALU.add)
                    ins.then_inc(y_used, 1)

            squares(0)
            for n in range(E + 1):
                if n < E:
                    squares(n + 1)
                if n:
                    v.wait_ge(y_used, 3 * n)
                add_expert(n)
            v.wait_ge(y_used, 3 * (E + 1))
            v.tensor_copy(s5[:, 3, :], s5[:, 2, :]).then_inc(h_ready, 2)

            for t in range(NT):
                stats(h, t)
            norm(xn, h, xn_ready)
            attention(1)

            norm(xn, h, xn_ready)
            v.wait_ge(xn_ready, 4 * NT)
            v.wait_ge(x3_act, 1)
            v.tensor_tensor(xr[:], xn[:], x3[:, 0], ALU.subtract).then_inc(x3_dve, 1)
            v.wait_ge(x3_act, 2)
            v.tensor_tensor(xr[:], xr[:], x3[:, 1], ALU.subtract).then_inc(x3_dve, 1)
            v.wait_ge(lg_ps, 2)
            done(v.tensor_copy(lg[:], ps[:, 4, 0:NT * E].rearrange("p (t e) -> p t e", e=E)))
            for t in range(NT):
                done(v.max(m8[:, t, :], lg[:, t, :]))
                mark(v.max_index(i8[:, t, :], m8[:, t, :], lg[:, t, :]))
            sync_own()
            v.tensor_tensor(ga[:], lg[:], m8[:, :, 0:1].broadcast_to(bc), ALU.subtract).then_inc(lg_ready, 1)
            done(v.tensor_copy(i8f[:], i8[:, :, 0:2]))
            v.tensor_tensor(ohb[:], it, i8f[:, :, 0:1].broadcast_to(bc), ALU.is_equal).then_inc(oh_ready, 1)
            v.wait_ge(ex_ready, 2)
            done(v.tensor_reduce(s5[:, 0, :], sg[:], AX_X, ALU.add))
            done(v.reciprocal(s5[:, 1, :], s5[:, 0, :]))
            v.wait_ge(cum_ps, 1)
            v.wait_ge(oh_ready, 1)
            done(v.tensor_tensor(gb[:], ps[:, 5, 0:NT * E].rearrange("p (t e) -> p t e", e=E), ohb[:], ALU.mult))
            done(v.tensor_reduce(s5[:, 2, :], gb[:], AX_X, ALU.add))
            done(v.tensor_scalar(s5[:, 0, :], s5[:, 2, :], float(CAP), float(4 * E * CAP), ALU.is_gt, ALU.mult))
            done(v.tensor_tensor(s5[:, 3, :], s5[:, 2, :], s5[:, 0, :], ALU.add))
            done(v.tensor_scalar(s5[:, 0, :], i8f[:, :, 0], float(CAP), -1.0, ALU.mult, ALU.add))
            done(v.tensor_tensor(s5[:, 2, :], s5[:, 3, :], s5[:, 0, :], ALU.add))
            v.wait_ge(ld["iota"], 16)
            for t in range(NT):
                v.tensor_scalar(sel[:, t, :], iota[:], s5[:, 2, t:t + 1], None, ALU.is_equal).then_inc(sel_ready, 1)
            for t in range(NT):
                v.tensor_scalar(dg[:, t, :], idn[:], s5[:, 2, t:t + 1], None, ALU.mult).then_inc(dg_ready, 1)
            v.wait_ge(slotb_ready, 2)
            for e in range(E):
                v.tensor_scalar(selT[0:CAP, e, :], slotb[:], c_("slot0", e)[0:CAP], None, ALU.is_equal)\
                 .then_inc(selT_ready, 1)
            v.wait_ge(ld["b2"], 16)
            for e in range(E):
                v.wait_ge(fy_ps, e + 1)
                v.tensor_tensor(ye[0:CAP, e, :], ps[0:CAP, 4 + e % 2, 0:D], b2r[0:CAP, e, :], ALU.add)\
                 .then_inc(ye_ready, 1)
            for t in range(NT):
                v.wait_ge(comb_ps, t + 1)
                v.scalar_tensor_tensor(out=res[:, t, :], in0=ps[:, (6 + t) % 8, 0:D], scalar=s5[:, 1, t:t + 1],
                                       in1=h[:, t, :], op0=ALU.mult, op1=ALU.add).then_inc(res_ready, 1)

        @block.tensor
        def _(pe):
            def product(out_ap, terms):
                for i, (w, x) in enumerate(terms):
                    ins = pe.matmul(out_ap, w, x, start=(i == 0), stop=(i == len(terms) - 1), skip_group_check=True)
                return ins

            pe.wait_ge(ld["idn"], 16)
            for g, (a, b) in enumerate(TOK_GROUPS):
                pe.wait_ge(pn_ready, b)
                for c in range(PC):
                    j = g * PC + c
                    if j >= 4:
                        pe.wait_ge(ztr_act if j % 2 == 0 else ztr_dve, (j - 4) // 2 + 1)
                    for t in range(a, b):
                        ins = pe.transpose(ps[:, j % 4, (t - a) * P:(t - a + 1) * P],
                                           tok[:, t, c * P:(c + 1) * P], idn[:])
                    ins.then_inc(ztr_ps, 1)
                pe.wait_ge(ztr_act, 3 * (g + 1))
                pe.wait_ge(ztr_dve, 3 * (g + 1))
                pe.wait_ge(ld["wz"], 16)
                for t in range(a, b):
                    product(ps[:, (4 + t) % 8, 0:D],
                            [(ztr[:, c, t * P:(t + 1) * P], wz[:, c, :]) for c in range(PC)]).then_inc(z_ps, 1)

            n_xn = [0]

            def xT_make():
                for g, (a, b) in enumerate(TOK_GROUPS):
                    pe.wait_ge(xn_ready, n_xn[0] * NT + b)
                    for c in range(KC):
                        for t in range(a, b):
                            ins = pe.transpose(ps[:, 2 * g + c, (t - a) * P:(t - a + 1) * P],
                                               xn[:, t, c * P:(c + 1) * P], idn[:])
                        ins.then_inc(xT_ps, 1)
                n_xn[0] += 1
                pe.wait_ge(xT_ready, 4 * n_xn[0])

            def attention(layer, w, wo, w_in, wo_in):
                xT_make()
                pe.wait_ge(w_in, 16)
                for i, base in enumerate((D, 0)):
                    for m in range(KC):
                        for half in range(2):
                            product(ps[:, 4 * i + 2 * m + half, 0:HALF],
                                    [(w[:, k, base + m * P:base + (m + 1) * P],
                                      xT[:, k, half * HALF:(half + 1) * HALF]) for k in range(KC)]).then_inc(qk_ps, 1)
                pe.wait_ge(kT_ready, 4 * layer + 4)
                for g in range(4):
                    for b in range(4 * g, 4 * g + 4):
                        for par in range(2):
                            c0 = 2 * D + par * P
                            ins = product(ps[par * SLOT:(par + 1) * SLOT, g, (b % 4) * P:(b % 4 + 1) * P],
                                          [(xT[:, k, b * T:b * T + SLOT], w[:, k, c0:c0 + P]) for k in range(KC)])
                    ins.then_inc(v_ps, 1)
                pe.wait_ge(qT_ready, 4 * layer + 4)
                if layer == 0:
                    pe.wait_ge(consts, 6)
                pe.wait_ge(ld["masks"], 48)
                for i in range(NPAIR + 3):
                    if i < NPAIR:
                        n = layer * NPAIR + i
                        if i >= 2:
                            pe.wait_ge(s_shifted, n - 1)
                        for m in range(KC):
                            if i == 0:
                                pe.wait_ge(kbd_dve, 2 * layer + m + 1)
                                pe.wait_ge(kbd_pool, 2 * layer + m + 1)
                            bank = 4 + 2 * (i % 2) + m
                            if layer == 1:
                                pe.matmul(ps[:, bank, 0:HM * T], spreadm[:], bandm[:], start=True, stop=False,
                                          skip_group_check=True)
                            for j in range(2):
                                b = 2 * i + j
                                ins = pe.matmul(ps[j * SLOT:(j + 1) * SLOT, bank, 0:HM * T],
                                                qT[:, m, b * T:b * T + SLOT], kbd[:, m, :, b * T:(b + 1) * T],
                                                start=(layer == 0), stop=True, skip_group_check=True)
                        ins.then_inc(s_ps, 1)
                    if 2 <= i < NPAIR + 2:
                        p = i - 2
                        n = layer * NPAIR + p
                        pe.wait_ge(pn, n + 1)
                        if p == 0:
                            pe.wait_ge(vbd_ready, 8 * layer + 8)
                        else:
                            pe.wait_ge(pT_ready, n)
                        for c in range(HM):
                            ins = pe.transpose(ps[:, c // 4, (c % 4) * P:(c % 4 + 1) * P],
                                               pe_[:, p % 3, 2 * c:2 * c + 2, :].rearrange("p h s -> p (h s)"), idn[:])
                        ins.then_inc(pT_ps, 1)
                    if i >= 3:
                        p = i - 3
                        n = layer * NPAIR + p
                        pe.wait_ge(pT_ready, n + 1)
                        if p >= 2:
                            pe.wait_ge(oT_ready, n - 1)
                        for j in range(2):
                            for c in range(HM):
                                q = slice(32 * (c % 4), 32 * (c % 4) + 32)
                                o = (c // 4) * 2 * T + j * T
                                ins = pe.matmul(ps[q, 2 + p % 2, o:o + T], vbd[:, 2 * p + j, c, :],
                                                pT[:, p % 2, c, j, :], start=True, stop=True, skip_group_check=True,
                                                tile_position=(0, 32 * (c % 4)))
                        ins.then_inc(o_ps, 1)
                pe.wait_ge(wo_in, 16)
                pe.wait_ge(oT_ready, (layer + 1) * NPAIR)
                for t in range(NT):
                    product(ps[:, (4 + t) % 8, 0:D],
                            [(oT[:, k, t * P:(t + 1) * P], wo[:, k, :]) for k in range(KC)]).then_inc(proj_ps, 1)

            def logits(w):
                for t in range(NT):
                    ins = product(ps[:, 4, t * E:(t + 1) * E],
                                  [(xT[:, k, t * P:(t + 1) * P], w[:, k, :]) for k in range(KC)])
                ins.then_inc(lg_ps, 1)

            attention(0, wqkv0, wo0, ld["wqkv0"], ld["wo0"])

            xT_make()
            pe.wait_ge(ld["gate"], 32)
            logits(gatew)

            def hidden(n):
                e = (n - 1) % (E + 1)
                pe.wait_ge(ld_moe[e], 16)
                for m in range(KC):
                    if n:
                        pe.wait_ge(relu_ready, 2 * n - 1 + m)
                    for half in range(2):
                        ins = product(ps[:, 2 * m + half, 0:HALF],
                                      [(wmoe[:, e, k, m * P:(m + 1) * P],
                                        xT[:, k, half * HALF:(half + 1) * HALF]) for k in range(KC)])
                    ins.then_inc(hid_ps, 1)

            def outputs(n):
                e = (n - 1) % (E + 1)
                pe.wait_ge(hid_ready, 2 * n + 2)
                for k, tiles in enumerate(((0, 1), (2, 3), (4,))):
                    if n:
                        pe.wait_ge(y_used, 3 * (n - 1) + k + 1)
                    for t in tiles:
                        m = min(P, N - t * P)
                        ins = product(ps[0:m, 5 + k, (t % 2) * D:(t % 2 + 1) * D],
                                      [(hid[:, n % 2, c, t * P:t * P + m], wmoe[:, e, KC + c, :]) for c in range(KC)])
                    ins.then_inc(y_ps, 1)

            hidden(0)
            for n in range(E + 1):
                if n < E:
                    hidden(n + 1)
                outputs(n)

            attention(1, wat1, wat1[:, :, 3 * D:4 * D], ld["wat1"], ld["wat1"])

            xT_make()
            logits(wgw)
            pe.wait_ge(oh_ready, 1)
            for t in range(NT):
                ins = product(ps[:, 5, t * E:(t + 1) * E],
                              [(upperm[:, 1, :], ohb[:, s, :]) for s in range(t)] + [(upperm[:, 0, :], ohb[:, t, :])])
            ins.then_inc(cum_ps, 1)
            pe.wait_ge(x3_act, 3)
            pe.wait_ge(sel_ready, NT)
            half_slots = E * CAP // 2
            for j in range(4):
                s, k = j // 2, j % 2
                product(ps[:, j, 0:half_slots],
                        [(x3[:, q, t, k * P:(k + 1) * P], sel[:, t, s * half_slots:(s + 1) * half_slots])
                         for t in range(NT) for q in range(3)]).then_inc(xg_ps, 1)
            for t in range(NT):
                pe.wait_ge(dg_ready, t + 1)
                ins = pe.matmul(ps[0:CAP, 6 + t // 4, (t % 4) * P:(t % 4 + 1) * P], onesm[:, 0:CAP], dg[:, t, :],
                                start=True, stop=True, skip_group_check=True)
                if t >= 3:
                    ins.then_inc(slotb_ps, 1)

            def up(e):
                pe.wait_ge(ld_f[e % RING], 32 * (e // RING + 1))
                pe.wait_ge(xg_ready, 2 if e == 0 else 4)
                if e >= 2:
                    pe.wait_ge(gelu_ready, 2 * (e - 1))
                for q in range(2):
                    for f in range(4 * q, 4 * q + 4):
                        ins = product(ps[:, 2 * (e % 2) + q, (f % 4) * CAP:(f % 4 + 1) * CAP],
                                      [(fw1[:, e % RING, k, f * P:(f + 1) * P], xg[:, k, e * CAP:(e + 1) * CAP])
                                       for k in range(KC)])
                    ins.then_inc(fh_ps, 1)

            def down(e):
                pe.wait_ge(gelu_ready, 2 * e + 2)
                if e >= 2:
                    pe.wait_ge(ye_ready, e - 1)
                product(ps[0:CAP, 4 + e % 2, 0:D],
                        [(hT[:, e % 2, f, :], fw2[:, e % RING, f, :]) for f in range(FC)]).then_inc(fy_ps, 1)

            up(0)
            for e in range(E):
                if e + 1 < E:
                    up(e + 1)
                down(e)
            pe.wait_ge(selT_ready, E)
            pe.wait_ge(ye_ready, E)
            for t in range(NT):
                product(ps[:, (6 + t) % 8, 0:D],
                        [(selT[0:CAP, e, t * P:(t + 1) * P], ye[0:CAP, e, :]) for e in range(E)]).then_inc(comb_ps, 1)


def layouts(x, cls_tok, L0_tok_ln1_g, L0_tok_ln1_b, L0_tok_W_proj, L0_tok_b_proj, L0_tok_ln2_g, L0_tok_ln2_b,
            L0_tok_cls_token, L0_tok_pos_emb, L0_attn_ln_gamma, L0_attn_ln_beta, L0_attn_W_qkv, L0_attn_b_qkv,
            L0_attn_W_proj, L0_attn_b_proj, L0_ffn_gate_w, L0_ffn_lb_bias, L0_ffn_w1, L0_ffn_w2, L0_ffn_cfc,
            L0_ffn_cproj, L1_attn_Wq, L1_attn_bq, L1_attn_Wk, L1_attn_bk, L1_attn_Wv, L1_attn_bv, L1_attn_Wo,
            L1_attn_bo, L1_ffn_wg, L1_ffn_W1, L1_ffn_b1, L1_ffn_W2, L1_ffn_b2):
    import numpy as np

    f32 = np.float32
    side = x.shape[2] // 6

    def by_token(a):
        a = np.concatenate([a.reshape(N, -1), np.zeros((NP - N, a.shape[-1]), f32)])
        return np.ascontiguousarray(a.reshape(NT, P, -1).transpose(1, 0, 2))

    def by_row(w):
        return np.ascontiguousarray(w.reshape(-1, P, w.shape[-1]).transpose(1, 0, 2))

    def by_col(a):
        return a.reshape(-1, P).T

    def odd_even(w):
        return w.reshape(w.shape[0], H // 2, 2, DH).transpose(0, 2, 1, 3).reshape(w.shape[0], D)

    pt = x.reshape(B, 3, 6, side, 6, side).transpose(0, 2, 4, 3, 5, 1).reshape(B, 36, PD)
    patches = by_token(np.concatenate([np.zeros((B, 2, PD), f32), pt], axis=1))
    wide = np.zeros((B, T, D), f32)
    scale_tok = wide.copy()
    scale_tok[:, 2:] = L0_tok_ln2_g
    shift_a = wide.copy()
    shift_a[:, 0] = cls_tok[0, 0]
    shift_a[:, 1:] = L0_tok_pos_emb[0]
    shift_b = wide.copy()
    shift_b[:, 1] = L0_tok_cls_token[0, 0]
    shift_b[:, 2:] = L0_tok_ln2_b
    w_qkv = by_row(np.concatenate([L0_attn_W_qkv[:, :2 * D], odd_even(L0_attn_W_qkv[:, 2 * D:])], axis=1))
    w_moe = np.stack([np.concatenate([by_row(a.T), by_row(b.T)], axis=1)
                      for a, b in [*zip(L0_ffn_w1, L0_ffn_w2), (L0_ffn_cfc, L0_ffn_cproj)]], axis=1)
    w_attn1 = by_row(np.concatenate([L1_attn_Wq.T, L1_attn_Wk.T, odd_even(L1_attn_Wv.T), L1_attn_Wo.T], axis=1))
    w1 = np.ascontiguousarray(L1_ffn_W1.reshape(E, KC, P, FF).transpose(2, 0, 1, 3))
    w2 = np.ascontiguousarray(L1_ffn_W2.reshape(E, FC, P, D).transpose(2, 0, 1, 3))
    bq0, bk0, bv0 = L0_attn_b_qkv.reshape(3, D)
    part = np.arange(P)
    head = (part[:, None] // DH == np.arange(HM)).astype(f32)
    slot0 = (part[:, None] + CAP * np.arange(E)).astype(f32)
    cols = np.concatenate([by_col(a) for a in (L0_tok_ln1_g, L0_tok_ln1_b, L0_attn_ln_gamma, L0_attn_ln_beta,
                                               bq0, bk0, bv0, L1_attn_bq, L1_attn_bk, L1_attn_bv, L1_ffn_b1)]
                          + [head, slot0], axis=1)
    rows = np.concatenate([L0_tok_b_proj, L0_attn_b_proj, L1_attn_bo, L0_ffn_lb_bias, np.arange(E).astype(f32)])
    near = np.abs(np.arange(T)[:, None] - np.arange(T)[None, :]) <= 3
    band = np.tile(np.where(near, 0.0, -1e30).astype(f32), (1, HM))
    spread = np.zeros((T, 2, SLOT), f32)
    spread[:, :, :T] = np.eye(T, dtype=f32)[:, None, :]
    upper = np.stack([np.triu(np.ones((P, P), f32)), np.ones((P, P), f32)], axis=1)
    bf = np.dtype("bfloat16")
    return {
        "patches": patches, "scale_tok": by_token(scale_tok), "shift_a": by_token(shift_a),
        "shift_b": by_token(shift_b), "w_patch": by_row(L0_tok_W_proj), "w_qkv": w_qkv,
        "w_out": by_row(L0_attn_W_proj), "gate": by_row(L0_ffn_gate_w.T), "w_moe": np.ascontiguousarray(w_moe),
        "w_attn1": w_attn1, "wg": by_row(L1_ffn_wg), "w1": w1, "w2": w2, "cols": np.ascontiguousarray(cols),
        "rows": np.ascontiguousarray(np.broadcast_to(rows, (P, NROWS))),
        "b2_rows": np.ascontiguousarray(np.broadcast_to(L1_ffn_b2, (P, E, D))),
        "iota_slots": np.ascontiguousarray(np.broadcast_to(np.arange(E * CAP, dtype=f32), (P, E * CAP))),
        "ident": np.eye(P, dtype=f32), "band": band.astype(bf), "spread": spread.reshape(T, P).astype(bf),
        "upper": upper.astype(bf),
    }


def kernel(**inputs):
    import numpy as np
    import concourse.bacc as bacc
    from concourse import mybir as mb
    from concourse.bass_utils import run_bass_kernel_spmd as run

    arrays = {f"in_{name}": a for name, a in layouts(**{k: np.asarray(v) for k, v in inputs.items()}).items()}
    nc = bacc.Bacc("TRN2", target_bir_lowering=False, num_devices=1)
    args = [nc.dram_tensor(name, a.shape, mb.dt.from_np(a.dtype), kind="ExternalInput").ap()
            for name, a in arrays.items()]
    result = nc.dram_tensor("out_0", (N, D), mb.dt.float32, kind="ExternalOutput").ap()
    vit_kernel(nc, *args, result)
    r = run(nc, [arrays], core_ids=[0])
    return r.results[0]["out_0"].reshape(B, T, D)
```

```python
import concourse.bass as bass
from concourse import mybir
from contextlib import ExitStack
from math import ceil

ALU = mybir.AluOpType
ACT = mybir.ActivationFunctionType
AX_X = mybir.AxisListType.X
F32 = mybir.dt.float32
F32R = mybir.dt.float32r
BF16 = mybir.dt.bfloat16
U32 = mybir.dt.uint32

P = 128
B = 16
T = 38
N = B * T
NT = 5
NP = NT * P
HALF = N // 2
D = 256
KC = D // P
PD = 768
PC = PD // P
H = 16
DH = D // H
HM = P // DH
NPAIR = B // 2
SLOT = 64
E = 8
CAP = int(N / E * 1.25) + 1
FF = 1024
FC = FF // P
SCALE = float(DH) ** -0.5
EPS = 1e-5
TOK_GROUPS = ((0, 2), (2, 4), (4, 5))
WARM = (30, 0, 0, 0)
RING = 3

COLS = {}
_at = 0
for _name, _n in (("ln1_g", PC), ("ln1_b", PC), ("lng", KC), ("lnb", KC),
                  ("bq0", KC), ("bk0", KC), ("bv0", KC), ("bq1", KC), ("bk1", KC), ("bv1", KC),
                  ("b1", E * FC), ("head", HM), ("slot0", E)):
    COLS[_name] = (_at, _at + _n)
    _at += _n
NCOLS = _at
ROWS = {}
_at = 0
for _name, _n in (("bz", D), ("bo0", D), ("bo1", D), ("lb", E), ("iota", E)):
    ROWS[_name] = (_at, _at + _n)
    _at += _n
NROWS = _at


def vit_kernel(nc, patches, scale_tok, shift_a, shift_b, w_patch, w_qkv, w_out, gate, w_moe, w_attn1, wg, w1, w2,
               cols, rows, b2_rows, iota_slots, ident, band, spread, upper, out):
    with ExitStack() as ctx:
        def sb(name, shape, dt=F32):
            return ctx.enter_context(nc.sbuf_tensor(name, shape, dt))

        def sem(name):
            return ctx.enter_context(nc.semaphore(name))

        def part(whole, at, shape, dt=F32):
            n = 1
            for x in shape:
                n *= x
            words = n // 2 if dt == BF16 else n
            ap = whole[:, at:at + words]
            if dt == BF16:
                ap = ap.bitcast(BF16)
            names = "abcd"[:len(shape)]
            spec = f"p ({' '.join(names)}) -> p {' '.join(names)}"
            return ap.rearrange(spec, **dict(zip(names, shape))), at + words

        ps = ctx.enter_context(nc.psum_tensor("ps", [P, 8, 512], F32))

        col = sb("col", [P, NCOLS])
        row = sb("row", [P, NROWS])
        idn = sb("idn", [P, P])
        bandm = sb("bandm", [T, HM * T], BF16)
        spreadm = sb("spreadm", [T, P], BF16)
        upperm = sb("upperm", [P, 2, P], BF16)
        onesm = sb("onesm", [P, P])
        neghalf = sb("neghalf", [P, NT])
        first_use = sb("first_use", [P, 2])
        wo0 = sb("wo0", [P, KC, D])
        gatew = sb("gatew", [P, KC, E])
        wgw = sb("wgw", [P, KC, E])
        wat1 = sb("wat1", [P, KC, 4 * D])
        weights = sb("weights", [P, RING * (KC * FF + FC * D)])
        wmoe, _ = part(weights, 0, [E + 1, 2 * KC, D])
        fw1, at = part(weights, 0, [RING, KC, FF])
        fw2, at = part(weights, at, [RING, FC, D])
        early = sb("early", [P, PC * D + KC * 3 * D])
        wz, at = part(early, 0, [PC, D])
        wqkv0, _ = part(early, at, [KC, 3 * D])
        b2r, at = part(early, 0, [E, D])
        iota, _ = part(early, at, [E * CAP])
        values = sb("values", [P, B * HM * 2 * DH])
        vbd, _ = part(values, 0, [B, HM, 2 * DH])
        xg, at = part(values, 0, [KC, E * CAP])
        hT, at = part(values, at, [2, FC, CAP])
        dg, at = part(values, at, [NT, P])
        zt = sb("zt", [P, NT, D])
        h = sb("h", [P, NT, D])
        hb = sb("hb", [P, NT, D])
        xn = sb("xn", [P, NT, D])
        xT = sb("xT", [P, KC, NP])
        qT = sb("qT", [P, KC, NP])
        kT = sb("kT", [P, KC, N])
        oT = sb("oT", [P, KC, NP])
        st = sb("st", [P, NT, 2, 6])
        mv = sb("mv", [P, NT, 2])
        ve = sb("ve", [P, NT])
        rstd = sb("rstd", [P, NT])
        sd = sb("sd", [P, 2, H, T])
        pe_ = sb("pe_", [P, 4, H, SLOT])
        mx = sb("mx", [P, 2, H])
        rs = sb("rs", [P, 2, H])
        ri = sb("ri", [P, 2, H])
        pT = sb("pT", [P, 2, HM, 2, T])
        lg = sb("lg", [P, NT, E])
        lgb = sb("lgb", [P, NT, E])
        m8 = sb("m8", [P, NT, 8])
        i8 = sb("i8", [P, NT, 8], U32)
        i8f = sb("i8f", [P, NT, 2])
        ga = sb("ga", [P, NT, E])
        gb = sb("gb", [P, NT, E])
        sg = sb("sg", [P, NT, E])
        we = sb("we", [P, NT, E])
        s5 = sb("s5", [P, 4, NT])
        ohb = sb("ohb", [P, NT, E], BF16)
        slotb = sb("slotb", [CAP, NP])
        rl = sd[:].rearrange("p a h t -> p (a h t)").rearrange("p (m h t) -> p m h t", m=2, h=2)
        hsq = pT[:].rearrange("p a h b t -> p (a h b t)").rearrange("p (m h t) -> p m h t", m=2, h=2)
        yt = hb
        res = zt

        with ExitStack() as stage:
            tok, ztr, gsc, sha, shb = (stage.enter_context(nc.sbuf_tensor(n, [P, *x], F32)) for n, x in (
                ("tok", (NT, PD)), ("ztr", (PC, NP)), ("gsc", (NT, D)), ("sha", (NT, D)), ("shb", (NT, D))))
        with ExitStack() as stage:
            kbd = stage.enter_context(nc.sbuf_tensor("kbd", [P, KC, HM, N], F32))
        with ExitStack() as stage:
            xh, xl, w1h, w1l, w2h, w2l, hh, hl = (
                stage.enter_context(nc.sbuf_tensor(n, [P, *x], F32R)) for n, x in (
                    ("xh", (KC, NP)), ("xl", (KC, NP)), ("w1h", (2, KC, D)), ("w1l", (2, KC, D)),
                    ("w2h", (2, KC, D)), ("w2l", (2, KC, D)), ("hh", (2, KC, N)), ("hl", (2, KC, N))))
        with ExitStack() as stage:
            selT = stage.enter_context(nc.sbuf_tensor("selT", [CAP, E, NP], F32R))
            with ExitStack() as inner:
                th, tl, sel = (inner.enter_context(nc.sbuf_tensor(n, [P, *x], F32R)) for n, x in (
                    ("th", (NT, D)), ("tl", (NT, D)), ("sel", (NT, E * CAP))))
            with ExitStack() as inner:
                yh, yl = (inner.enter_context(nc.sbuf_tensor(n, [CAP, E, D], F32R)) for n in ("yh", "yl"))

        def c_(name, i=0, n=1):
            return col[:, COLS[name][0] + i:COLS[name][0] + i + n]

        def r_(name):
            return row[:, ROWS[name][0]:ROWS[name][1]]

        ld_tok = [sem(f"ld_tok{t}") for t in range(NT)]
        ld = {n: sem("ld_" + n) for n in ("col", "row", "b2", "iota", "idn", "masks", "wz", "gsc", "shift", "wqkv0", "wo0",
                                          "gate", "wat1")}
        ld_moe = [sem(f"ld_moe{e}") for e in range(E + 1)]
        ld_f1 = [sem(f"ld_f1_{r}") for r in range(RING)]
        ld_f2 = [sem(f"ld_f2_{r}") for r in range(RING)]
        consts = sem("consts")
        dve = sem("dve")
        var_ready = sem("var_ready")
        rstd_ready = sem("rstd_ready")
        pn_ready = sem("pn_ready")
        ztr_ps = sem("ztr_ps")
        ztr_ready = sem("ztr_ready")
        z_ps = sem("z_ps")
        shift_ready = sem("shift_ready")
        h_ready = sem("h_ready")
        hb_ready = sem("hb_ready")
        xn_ready = sem("xn_ready")
        xT_ps = sem("xT_ps")
        xT_ready = sem("xT_ready")
        xl_ready = sem("xl_ready")
        qk_ps = sem("qk_ps")
        kT_ready = sem("kT_ready")
        qT_ready = sem("qT_ready")
        kbd_dve = sem("kbd_dve")
        kbd_pool = sem("kbd_pool")
        v_ps = sem("v_ps")
        vbd_ready = sem("vbd_ready")
        s_ps = sem("s_ps")
        s_shifted = sem("s_shifted")
        exp_ready = sem("exp_ready")
        rs_ready = sem("rs_ready")
        pn = sem("pn")
        pT_ps = sem("pT_ps")
        pT_ready = sem("pT_ready")
        o_ps = sem("o_ps")
        oT_ready = sem("oT_ready")
        proj_ps = sem("proj_ps")
        lg_ps = sem("lg_ps")
        lg_ready = sem("lg_ready")
        ex_ready = sem("ex_ready")
        hid_ps = sem("hid_ps")
        relu_ready = sem("relu_ready")
        hh_ready = sem("hh_ready")
        hl_ready = sem("hl_ready")
        y_ps = sem("y_ps")
        y_used = sem("y_used")
        w1h_ready = sem("w1h_ready")
        w1l_ready = sem("w1l_ready")
        w2h_ready = sem("w2h_ready")
        w2l_ready = sem("w2l_ready")
        th_ready = sem("th_ready")
        tl_ready = sem("tl_ready")
        oh_ready = sem("oh_ready")
        cum_ps = sem("cum_ps")
        dg_ready = sem("dg_ready")
        slotb_ps = sem("slotb_ps")
        slotb_ready = sem("slotb_ready")
        sel_ready = sem("sel_ready")
        selT_ready = sem("selT_ready")
        xg_ps = sem("xg_ps")
        xg_ready = sem("xg_ready")
        fh_ps = sem("fh_ps")
        gelu_ready = sem("gelu_ready")
        fy_ps = sem("fy_ps")
        yt_ready = sem("yt_ready")
        yh_ready = sem("yh_ready")
        yl_ready = sem("yl_ready")
        comb_ps = sem("comb_ps")
        res_ready = sem("res_ready")
        stored = sem("stored")

        Y_BANKS = ((0, 1), (2, 3), (4,))
        Z_BANKS = (4, 5, 6, 7, 3)
        half_slots = E * CAP // 2

        def expert(n):
            return (n - 1) % (E + 1)

        block = ctx.enter_context(nc.Block())

        @block.sync
        def _(sp):
            def load(dst, src, s):
                sp.dma_start(dst, src).then_inc(s, 16)

            for t in range(2):
                load(tok[:, t, :], patches[:, t, :], ld_tok[t])
            load(idn[:], ident, ld["idn"])
            load(col[:], cols, ld["col"])
            for t in range(2, NT):
                load(tok[:, t, :], patches[:, t, :], ld_tok[t])
            load(wz[:], w_patch, ld["wz"])
            load(row[:], rows, ld["row"])
            load(gsc[:], scale_tok, ld["gsc"])
            load(sha[:], shift_a, ld["shift"])
            load(shb[:], shift_b, ld["shift"])
            load(wqkv0[:], w_qkv, ld["wqkv0"])
            load(bandm[:], band, ld["masks"])
            load(spreadm[:], spread, ld["masks"])
            load(upperm[:], upper, ld["masks"])
            load(wo0[:], w_out, ld["wo0"])
            load(gatew[:], gate, ld["gate"])
            load(wgw[:], wg, ld["gate"])
            for n in range(E + 1):
                load(wmoe[:, expert(n)], w_moe[:, expert(n)], ld_moe[expert(n)])
            load(wat1[:], w_attn1, ld["wat1"])
            sp.wait_ge(w1l_ready, E + 1)
            sp.wait_ge(w2l_ready, E + 1)
            load(iota[:], iota_slots, ld["iota"])
            load(b2r[:], b2_rows, ld["b2"])
            for e in range(E):
                if e >= RING:
                    sp.wait_ge(fh_ps, 2 * (e - RING + 1))
                load(fw1[:, e % RING], w1[:, e], ld_f1[e % RING])
                if e >= RING:
                    sp.wait_ge(fy_ps, e - RING + 1)
                load(fw2[:, e % RING], w2[:, e], ld_f2[e % RING])
            for t in range(NT):
                n = min(P, N - t * P)
                sp.wait_ge(res_ready, t + 1)
                sp.dma_start(out[t * P:t * P + n, :], res[0:n, t, :]).then_inc(stored, 16)
            sp.wait_ge(stored, 16 * NT)

        @block.gpsimd
        def _(gp):
            gp.memset(neghalf[:], -0.5).then_inc(consts, 1)
            gp.memset(onesm[:], 1.0).then_inc(consts, 1)
            gp.memset(vbd[:], 0.0).then_inc(consts, 1)
            gp.wait_ge(consts, 1)
            n_rstd = [0]

            def rstd_step(t):
                n_rstd[0] += 1
                gp.wait_ge(var_ready, n_rstd[0])
                gp.tensor_tensor(rstd[:, t:t + 1], ve[:, t:t + 1], neghalf[:, t:t + 1], ALU.pow)\
                  .then_inc(rstd_ready, 1)

            for t in range(NT):
                rstd_step(t)
            gp.memset(qT[:, :, N:NP], 0.0).then_inc(consts, 1)
            gp.memset(oT[:, :, N:NP], 0.0).then_inc(consts, 1)
            gp.memset(pe_[:], 0.0).then_inc(consts, 1)
            gp.wait_ge(ld["shift"], 32)
            for t in range(NT):
                gp.tensor_tensor(shb[:, t, :], sha[:, t, :], shb[:, t, :], ALU.add).then_inc(shift_ready, 1)
            for step in range(NT + 1):
                for lag in (1, 0):
                    if 0 <= step - lag < NT:
                        rstd_step(step - lag)

            def add_bias(name, n):
                gp.wait_ge(h_ready, NT * n)
                for t in range(NT):
                    gp.tensor_tensor(hb[:, t, :], h[:, t, :], r_(name), ALU.add).then_inc(hb_ready, 1)

            def attention(layer):
                for m in range(KC):
                    gp.wait_ge(kT_ready, 4 * layer + 3 + m)
                    for hh_ in range(HM // 2, HM):
                        ins = gp.tensor_scalar(kbd[:, m, hh_, :], kT[:, m, :], c_("head", hh_), 1.0,
                                               ALU.mult, ALU.mult)
                    ins.then_inc(kbd_pool, 1)
                for p in range(NPAIR):
                    gp.wait_ge(rs_ready, layer * NPAIR + p + 1)
                    w = pe_[:, p % 4, :, 0:T]
                    gp.tensor_tensor(w, w, ri[:, p % 2, :].unsqueeze(2).broadcast_to([P, H, T]), ALU.mult)\
                      .then_inc(pn, 1)

            def low_part(n, k, dst, high_, high_ready, ready):
                gp.wait_ge(high_ready, n + 1)
                gp.tensor_tensor(dst[:, n % 2], wmoe[:, expert(n), k * KC:(k + 1) * KC, :],
                                 high_[:, n % 2].bitcast(F32), ALU.subtract).then_inc(ready, 1)

            add_bias("bo0", 1)
            attention(0)
            low_part(0, 0, w1l, w1h, w1h_ready, w1l_ready)
            for t in range(NT):
                rstd_step(t)
            low_part(1, 0, w1l, w1h, w1h_ready, w1l_ready)
            low_part(0, 1, w2l, w2h, w2h_ready, w2l_ready)
            for n in range(E + 1):
                if n + 2 <= E:
                    low_part(n + 2, 0, w1l, w1h, w1h_ready, w1l_ready)
                if n + 1 <= E:
                    low_part(n + 1, 1, w2l, w2h, w2h_ready, w2l_ready)
            for t in range(NT):
                rstd_step(t)
            add_bias("bo1", 2)
            attention(1)
            for t in range(NT):
                rstd_step(t)
            gp.wait_ge(th_ready, 1)
            gp.tensor_tensor(tl[:], xn[:], th[:].bitcast(F32), ALU.subtract).then_inc(tl_ready, 1)

        @block.scalar
        def _(sc):
            sc.wait_ge(consts, 1)
            sc.activation(first_use[:, 0:1], neghalf[:, 0:1], ACT.Exp)
            sc.wait_ge(ld["col"], 16)
            for g, (a, b) in enumerate(TOK_GROUPS):
                for i in range(PC // 2):
                    j = g * (PC // 2) + i
                    sc.wait_ge(ztr_ps, j + 1)
                    for c in (2 * i, 2 * i + 1):
                        w = (b - a) * P
                        ins = sc.activation(ztr[:, c, a * P:b * P], ps[:, j % 3, (c % 2) * w:(c % 2 + 1) * w],
                                            ACT.Identity, scale=c_("ln1_g", c), bias=c_("ln1_b", c))
                    ins.then_inc(ztr_ready, 1)

            def bank_of_group(g):
                a, b = TOK_GROUPS[g]
                return ps[:, g, 0:KC * (b - a) * P].rearrange("p (c n) -> p c n", c=KC)

            n_xT = [0]

            def xT_evict(kind):
                for g, (a, b) in enumerate(TOK_GROUPS):
                    n_xT[0] += 1
                    sc.wait_ge(xT_ps, n_xT[0])
                    src = bank_of_group(g)
                    if kind == "affine":
                        for c in range(KC):
                            ins = sc.activation(xT[:, c, a * P:b * P], src[:, c, :], ACT.Identity,
                                                scale=c_("lng", c), bias=c_("lnb", c))
                    else:
                        if kind == "split":
                            sc.activation(xh[:, :, a * P:b * P], src, ACT.Copy)
                        ins = sc.activation(xT[:, :, a * P:b * P], src, ACT.Copy)
                    ins.then_inc(xT_ready, 1)

            def attention(layer):
                xT_evict("whole" if layer else "affine")
                for i, (dst, name, ready) in enumerate(((kT, "bk", kT_ready), (qT, "bq", qT_ready))):
                    for half in range(2):
                        for m in range(KC):
                            n = 4 * i + 2 * half + m
                            sc.wait_ge(qk_ps, 8 * layer + n + 1)
                            sc.activation(dst[:, m, half * HALF:(half + 1) * HALF], ps[:, n, 0:HALF],
                                          ACT.Identity, bias=c_(f"{name}{layer}", m)).then_inc(ready, 1)
                for i in range(NPAIR + 4):
                    n = layer * NPAIR + i
                    if 3 <= i < NPAIR + 3:
                        sc.wait_ge(pT_ps, n - 3 + 1)
                        if i - 3 >= 2:
                            sc.wait_ge(o_ps, n - 3 - 1)
                        src = ps[:, 0:2, :].rearrange("p k (h b s) -> p (k h) b s", h=4, b=2)
                        sc.copy(pT[:, (i - 3) % 2], src[:, :, :, 0:T]).then_inc(pT_ready, 1)
                    if i < NPAIR:
                        sc.wait_ge(s_shifted, n + 1)
                        if i >= 4:
                            sc.wait_ge(pT_ps, n - 4 + 1)
                        elif layer == 0:
                            sc.wait_ge(consts, 6)
                        sc.activation(pe_[:, i % 4, :, 0:T], sd[:, i % 2], ACT.Exp, scale=SCALE)\
                          .then_inc(exp_ready, 1)
                    if i == 1:
                        for g in range(4):
                            sc.wait_ge(v_ps, 4 * layer + g + 1)
                            for par in range(2):
                                q = slice(par * SLOT, (par + 1) * SLOT)
                                src = ps[q, g, :].rearrange("p (b h d) -> p b h d", b=4, h=HM)
                                sc.copy(vbd[q, 4 * g:4 * g + 4, :, par * DH:(par + 1) * DH], src)\
                                  .then_inc(vbd_ready, 1)
                    if i >= 4:
                        p = i - 4
                        sc.wait_ge(o_ps, n - 4 + 1)
                        for m in range(KC):
                            ins = sc.activation(oT[:, m, p * 2 * T:(p + 1) * 2 * T],
                                                ps[:, 2 + p % 2, m * 2 * T:(m + 1) * 2 * T], ACT.Identity,
                                                bias=c_(f"bv{layer}", m))
                        ins.then_inc(oT_ready, 1)

            def high_part(n, k, dst, used, ready):
                if n == 0 or k == 0 and n == 1:
                    pass
                else:
                    sc.wait_ge(*used)
                sc.wait_ge(ld_moe[expert(n)], 16)
                sc.activation(dst[:, n % 2], wmoe[:, expert(n), k * KC:(k + 1) * KC, :], ACT.Copy).then_inc(ready, 1)

            attention(0)
            high_part(0, 0, w1h, None, w1h_ready)
            high_part(1, 0, w1h, None, w1h_ready)
            high_part(0, 1, w2h, None, w2h_ready)
            xT_evict("split")
            for n in range(E + 1):
                for m in range(KC):
                    sc.wait_ge(hid_ps, 2 * n + m + 1)
                    if n:
                        sc.wait_ge(hl_ready, 2 * n - 1 + m)
                    sc.activation(rl[:, m], ps[:, 2 * m:2 * m + 2, 0:HALF], ACT.Relu).then_inc(relu_ready, 1)
                    sc.wait_ge(relu_ready, 2 * n + m + 1)
                    if n >= 2:
                        sc.wait_ge(y_ps, 3 * (n - 1))
                    sc.activation(hh[:, n % 2, m, :].rearrange("p (a b) -> p a b", a=2), rl[:, m], ACT.Square)\
                      .then_inc(hh_ready, 1)
                if n == 0:
                    sc.wait_ge(lg_ready, 1)
                    sc.activation(sg[:], lg[:], ACT.Exp, scale=-1.0).then_inc(ex_ready, 1)
                if n + 2 <= E:
                    high_part(n + 2, 0, w1h, (hid_ps, 2 * n + 2), w1h_ready)
                if n + 1 <= E:
                    high_part(n + 1, 1, w2h, (y_ps, 3 * n), w2h_ready)
            attention(1)
            xT_evict("whole")
            sc.wait_ge(xn_ready, 4 * NT)
            sc.activation(th[:], xn[:], ACT.Copy).then_inc(th_ready, 1)
            sc.wait_ge(lg_ready, 2)
            sc.activation(sg[:], ga[:], ACT.Exp).then_inc(ex_ready, 1)
            sc.activation(first_use[:, 1:2], neghalf[:, 0:1], ACT.Gelu)
            for j in range(4):
                sc.wait_ge(xg_ps, j + 1)
                s = j // 2
                sc.copy(xg[:, j % 2, s * half_slots:(s + 1) * half_slots], ps[:, j, 0:half_slots])\
                  .then_inc(xg_ready, 1)
            for i, (a, b) in enumerate(((0, 512), (512, NP))):
                sc.wait_ge(slotb_ps, i + 1)
                sc.copy(slotb[:, a:b], ps[0:CAP, 6 + i, 0:b - a]).then_inc(slotb_ready, 1)

            def high_y(e):
                sc.wait_ge(yt_ready, e + 1)
                sc.activation(yh[:, e, :], yt[0:CAP, e % 2, :], ACT.Copy).then_inc(yh_ready, 1)

            for e in range(E):
                for q in range(2):
                    sc.wait_ge(fh_ps, 2 * e + q + 1)
                    if e >= 2 and q == 0:
                        sc.wait_ge(fy_ps, e - 1)
                    for f in range(4 * q, 4 * q + 4):
                        ins = sc.activation(hT[:, e % 2, f, :], ps[:, 2 * (e % 2) + q, (f % 4) * CAP:(f % 4 + 1) * CAP],
                                            ACT.Gelu, bias=c_("b1", e * FC + f))
                    ins.then_inc(gelu_ready, 1)
                if e:
                    high_y(e - 1)
            high_y(E - 1)

        @block.vector
        def _(v):
            own = [0]

            def mark(ins):
                own[0] += 1
                ins.then_inc(dve, 1)

            def settle():
                v.wait_ge(dve, own[0])

            def done(ins):
                mark(ins)
                settle()

            n_rstd = [0]

            def next_rstd():
                n_rstd[0] += 1
                v.wait_ge(rstd_ready, n_rstd[0])

            def stats(src, t, twice=False):
                settle()
                done(v.bn_stats(st[:, t, 0, :], src))
                done(v.bn_aggr(mv[:, t, :], st[:, t, 0, :]))
                a, b = (1.0 + EPS, EPS * EPS) if twice else (1.0, EPS)
                v.tensor_scalar(ve[:, t:t + 1], mv[:, t, 1:2], a, b, ALU.mult, ALU.add).then_inc(var_ready, 1)

            def centre(dst, src, t):
                next_rstd()
                return v.tensor_scalar(dst[:, t, :], src[:, t, :], mv[:, t, 0:1], rstd[:, t:t + 1],
                                       ALU.subtract, ALU.mult)

            def patch_stats(t):
                v.wait_ge(ld_tok[t], 16)
                for k in range(2):
                    mark(v.bn_stats(st[:, t, k, :], tok[:, t, k * (PD // 2):(k + 1) * (PD // 2)]))
                settle()
                done(v.bn_aggr(mv[:, t, :], st[:, t].rearrange("p k s -> p (k s)")))
                v.tensor_scalar(ve[:, t:t + 1], mv[:, t, 1:2], EPS, None, ALU.add).then_inc(var_ready, 1)

            patch_stats(0)
            for t in range(NT):
                if t + 1 < NT:
                    patch_stats(t + 1)
                centre(tok, tok, t).then_inc(pn_ready, 1)

            v.wait_ge(ld["gsc"], 16)
            for step in range(NT + 2):
                t = step - 2
                if 0 <= t < NT:
                    centre(xn, h, t).then_inc(xn_ready, 1)
                t = step - 1
                if 0 <= t < NT:
                    done(v.scalar_tensor_tensor(out=zt[:, t, :], in0=ps[:, Z_BANKS[t], 0:D], scalar=mv[:, t, 0:1],
                                                in1=gsc[:, t, :], op0=ALU.subtract, op1=ALU.mult))
                    next_rstd()
                    v.wait_ge(shift_ready, t + 1)
                    v.scalar_tensor_tensor(out=h[:, t, :], in0=zt[:, t, :], scalar=rstd[:, t:t + 1],
                                           in1=shb[:, t, :], op0=ALU.mult, op1=ALU.add).then_inc(h_ready, 1)
                    v.wait_ge(h_ready, t + 1)
                    stats(h[:, t, :], t, twice=True)
                t = step
                if t < NT:
                    v.wait_ge(z_ps, t + 1)
                    stats(ps[:, Z_BANKS[t], 0:D], t)

            def attention(layer):
                for m in range(KC):
                    v.wait_ge(kT_ready, 4 * layer + 3 + m)
                    for hh_ in range(HM // 2):
                        ins = v.tensor_scalar(kbd[:, m, hh_, :], kT[:, m, :], c_("head", hh_), None, ALU.mult)
                    ins.then_inc(kbd_dve, 1)
                for i in range(NPAIR + 1):
                    if i < NPAIR:
                        n = layer * NPAIR + i
                        v.wait_ge(s_ps, n + 1)
                        s = ps[:, 4 + 2 * (i % 2):6 + 2 * (i % 2), 0:HM * T].rearrange("p m (h k) -> p m h k", h=HM)
                        done(v.tensor_reduce(mx[:, i % 2, :].rearrange("p (m h) -> p m h", m=KC), s, AX_X, ALU.max))
                        if i >= 2:
                            v.wait_ge(exp_ready, n - 1)
                        mb = mx[:, i % 2, :].rearrange("p (m h) -> p m h", m=KC).unsqueeze(3)
                        v.tensor_tensor(sd[:, i % 2].rearrange("p (m h) k -> p m h k", m=KC), s,
                                        mb.broadcast_to([P, KC, HM, T]), ALU.subtract).then_inc(s_shifted, 1)
                    if i >= 1:
                        p = i - 1
                        v.wait_ge(exp_ready, layer * NPAIR + p + 1)
                        done(v.tensor_reduce(rs[:, p % 2, :], pe_[:, p % 4, :, 0:T], AX_X, ALU.add))
                        if p >= 2:
                            v.wait_ge(pn, layer * NPAIR + p - 1)
                        v.reciprocal(ri[:, p % 2, :], rs[:, p % 2, :]).then_inc(rs_ready, 1)
                for step in range(NT + 1):
                    t = step
                    if t < NT:
                        v.wait_ge(proj_ps, layer * NT + t + 1)
                        v.wait_ge(hb_ready, layer * NT + t + 1)
                        mark(v.tensor_tensor(h[:, t, :], ps[:, Z_BANKS[t], 0:D], hb[:, t, :], ALU.add))
                        stats(h[:, t, :], t)
                    if step:
                        centre(xn, h, step - 1).then_inc(xn_ready, 1)

            attention(0)

            for g, (a, b) in enumerate(TOK_GROUPS):
                v.wait_ge(xT_ready, len(TOK_GROUPS) + g + 1)
                v.tensor_tensor(xl[:, :, a * P:b * P], xT[:, :, a * P:b * P], xh[:, :, a * P:b * P].bitcast(F32),
                                ALU.subtract)\
                 .then_inc(xl_ready, 1)
            bc = [P, NT, E]
            it = r_("iota").unsqueeze(1).broadcast_to(bc)

            def choices(x):
                for t in range(NT):
                    mark(v.max(m8[:, t, :], x[:, t, :]))
                settle()
                for t in range(NT):
                    mark(v.max_index(i8[:, t, :], m8[:, t, :], x[:, t, :]))

            def gates():
                v.wait_ge(lg_ready, 1)
                done(v.tensor_tensor(lgb[:], lg[:], r_("lb").unsqueeze(1).broadcast_to(bc), ALU.add))
                choices(lgb)
                settle()
                done(v.tensor_copy(i8f[:], i8[:, :, 0:2]))
                mark(v.tensor_tensor(ga[:], it, i8f[:, :, 0:1].broadcast_to(bc), ALU.is_equal))
                done(v.tensor_tensor(gb[:], it, i8f[:, :, 1:2].broadcast_to(bc), ALU.is_equal))
                done(v.tensor_tensor(ga[:], ga[:], gb[:], ALU.add))
                v.wait_ge(ex_ready, 1)
                done(v.tensor_scalar(gb[:], sg[:], 1.0, None, ALU.add))
                done(v.reciprocal(sg[:], gb[:]))
                done(v.tensor_tensor(gb[:], sg[:], ga[:], ALU.mult))
                done(v.tensor_reduce(s5[:, 0, :], gb[:], AX_X, ALU.add))
                done(v.tensor_scalar(s5[:, 1, :], s5[:, 0, :], 1e-6, None, ALU.add))
                done(v.reciprocal(s5[:, 2, :], s5[:, 1, :]))
                done(v.tensor_tensor(we[:], gb[:], s5[:, 2, :].unsqueeze(2).broadcast_to(bc), ALU.mult))

            def squares(n):
                for m in range(KC):
                    v.wait_ge(relu_ready, 2 * n + m + 1)
                    done(v.tensor_tensor(hsq[:, m], rl[:, m], rl[:, m], ALU.mult))
                    v.wait_ge(hh_ready, 2 * n + m + 1)
                    if n >= 2 and m == 0:
                        v.wait_ge(y_ps, 3 * (n - 1))
                    v.tensor_tensor(hl[:, n % 2, m, :].rearrange("p (a b) -> p a b", a=2), hsq[:, m],
                                    hh[:, n % 2, m, :].rearrange("p (a b) -> p a b", a=2).bitcast(F32),
                                    ALU.subtract).then_inc(hl_ready, 1)

            def add_expert(n):
                for k, tiles in enumerate(Y_BANKS):
                    v.wait_ge(y_ps, 3 * n + k + 1)
                    if n:
                        v.wait_ge(y_used, 3 * (n - 1) + k + 1)
                    for t in tiles:
                        m = min(P, N - t * P)
                        y = ps[0:m, 5 + k, (t % 2) * D:(t % 2 + 1) * D]
                        if n == 0:
                            ins = v.tensor_tensor(h[0:m, t, :], y, h[0:m, t, :], ALU.add)
                        else:
                            ins = v.scalar_tensor_tensor(out=h[0:m, t, :], in0=y, scalar=we[0:m, t, n - 1:n],
                                                         in1=h[0:m, t, :], op0=ALU.mult, op1=ALU.add)
                        if n == E:
                            ins.then_inc(h_ready, 1)
                            v.wait_ge(h_ready, NT + t + 1)
                            stats(h[:, t, :], t)
                            if t:
                                centre(xn, h, t - 1).then_inc(xn_ready, 1)
                        elif t == tiles[-1]:
                            ins.then_inc(y_used, 1)

            v.wait_ge(lg_ps, 1)
            v.tensor_copy(lg[:], ps[:, 4, 0:NT * E].rearrange("p (t e) -> p t e", e=E)).then_inc(lg_ready, 1)
            squares(0)
            gates()
            for n in range(E + 1):
                if n < E:
                    squares(n + 1)
                add_expert(n)
            centre(xn, h, NT - 1).then_inc(xn_ready, 1)

            attention(1)

            v.wait_ge(lg_ps, 2)
            done(v.tensor_copy(lg[:], ps[:, 4, 0:NT * E].rearrange("p (t e) -> p t e", e=E)))
            choices(lg)
            settle()
            done(v.tensor_copy(i8f[:], i8[:, :, 0:2]))
            v.tensor_tensor(ohb[:], it, i8f[:, :, 0:1].broadcast_to(bc), ALU.is_equal).then_inc(oh_ready, 1)
            v.tensor_tensor(ga[:], lg[:], m8[:, :, 0:1].broadcast_to(bc), ALU.subtract).then_inc(lg_ready, 1)
            done(v.tensor_scalar(s5[:, 3, :], i8f[:, :, 0], float(CAP), -1.0, ALU.mult, ALU.add))
            v.wait_ge(cum_ps, 1)
            v.wait_ge(oh_ready, 1)
            done(v.tensor_tensor(gb[:], ps[:, 5, 0:NT * E].rearrange("p (t e) -> p t e", e=E), ohb[:], ALU.mult))
            done(v.tensor_reduce(s5[:, 2, :], gb[:], AX_X, ALU.add))
            mark(v.tensor_tensor(s5[:, 1, :], s5[:, 2, :], s5[:, 3, :], ALU.add))
            done(v.tensor_scalar(s5[:, 0, :], s5[:, 2, :], float(CAP), float(4 * E * CAP), ALU.is_gt, ALU.mult))
            done(v.tensor_tensor(s5[:, 2, :], s5[:, 1, :], s5[:, 0, :], ALU.add))
            v.wait_ge(ld["iota"], 16)
            for t in range(NT):
                v.tensor_scalar(sel[:, t, :], iota[:], s5[:, 2, t:t + 1], None, ALU.is_equal).then_inc(sel_ready, 1)
            for t in range(NT):
                v.tensor_scalar(dg[:, t, :], idn[:], s5[:, 2, t:t + 1], None, ALU.mult).then_inc(dg_ready, 1)
            v.wait_ge(ex_ready, 2)
            done(v.tensor_reduce(s5[:, 0, :], sg[:], AX_X, ALU.add))
            done(v.reciprocal(s5[:, 1, :], s5[:, 0, :]))
            v.wait_ge(slotb_ready, 2)
            for e in range(E):
                v.tensor_scalar(selT[:, e, :], slotb[:], c_("slot0", e)[0:CAP], None, ALU.is_equal)\
                 .then_inc(selT_ready, 1)
            v.wait_ge(ld["b2"], 16)
            v.wait_ge(xg_ps, 4)
            for e in range(E):
                v.wait_ge(fy_ps, e + 1)
                v.tensor_tensor(yt[0:CAP, e % 2, :], ps[0:CAP, 4 + e % 2, 0:D], b2r[0:CAP, e, :], ALU.add)\
                 .then_inc(yt_ready, 1)
                v.wait_ge(yh_ready, e + 1)
                v.tensor_tensor(yl[:, e, :], yt[0:CAP, e % 2, :], yh[:, e, :].bitcast(F32), ALU.subtract)\
                 .then_inc(yl_ready, 1)
            for t in range(NT):
                v.wait_ge(comb_ps, t + 1)
                v.scalar_tensor_tensor(out=res[:, t, :], in0=ps[:, (6, 7, 0, 1, 2)[t], 0:D], scalar=s5[:, 1, t:t + 1],
                                       in1=h[:, t, :], op0=ALU.mult, op1=ALU.add).then_inc(res_ready, 1)

        @block.tensor
        def _(pe):
            def product(out_ap, terms):
                for i, (w, x) in enumerate(terms):
                    ins = pe.matmul(out_ap, w, x, start=(i == 0), stop=(i == len(terms) - 1), skip_group_check=True)
                return ins

            def split_terms(w_parts, x_parts):
                (wh, wl), (xh_, xl_) = w_parts, x_parts
                return [(wh, xh_), (wh, xl_), (wl, xh_)]

            def keep_warm(n, bank, col_):
                for _ in range(n):
                    pe.matmul(ps[:, bank, col_:col_ + P], onesm[:], onesm[:], start=True, stop=True,
                              skip_group_check=True)

            pe.wait_ge(consts, 2)
            keep_warm(WARM[0], 0, 0)
            pe.wait_ge(ld["idn"], 16)
            steps = [(g, i) for g in range(len(TOK_GROUPS)) for i in range(PC // 2)]
            for j in range(len(steps) + 3):
                if j >= 3:
                    g, i = steps[j - 3]
                    a, b = TOK_GROUPS[g]
                    if i == 0:
                        pe.wait_ge(ld["row"], 16)
                        for t in range(a, b):
                            pe.matmul(ps[:, Z_BANKS[t], 0:D], onesm[0:1, :], r_("bz")[0:1, :], start=True, stop=False,
                                      skip_group_check=True)
                    pe.wait_ge(ld["wz"], 16)
                    pe.wait_ge(ztr_ready, j - 2)
                    for t in range(a, b):
                        for c in (2 * i, 2 * i + 1):
                            ins = pe.matmul(ps[:, Z_BANKS[t], 0:D], ztr[:, c, t * P:(t + 1) * P], wz[:, c, :],
                                            start=False, stop=(c == PC - 1), skip_group_check=True)
                        if i == PC // 2 - 1:
                            ins.then_inc(z_ps, 1)
                if j < len(steps):
                    g, i = steps[j]
                    a, b = TOK_GROUPS[g]
                    pe.wait_ge(pn_ready, b)
                    w = (b - a) * P
                    for c in (2 * i, 2 * i + 1):
                        for t in range(a, b):
                            ins = pe.transpose(ps[:, j % 3, (c % 2) * w + (t - a) * P:(c % 2) * w + (t - a + 1) * P],
                                               tok[:, t, c * P:(c + 1) * P], idn[:])
                    ins.then_inc(ztr_ps, 1)

            n_xn = [0]

            def logits(g, w):
                pe.wait_ge(ld["gate"], 32)
                pe.wait_ge(xT_ready, len(TOK_GROUPS) * n_xn[0] + g + 1)
                for t in range(*TOK_GROUPS[g]):
                    ins = product(ps[:, 4, t * E:(t + 1) * E],
                                  [(xT[:, k, t * P:(t + 1) * P], w[:, k, :]) for k in range(KC)])
                if t == NT - 1:
                    ins.then_inc(lg_ps, 1)

            def xT_make(gate_w=None):
                for g, (a, b) in enumerate(TOK_GROUPS):
                    pe.wait_ge(xn_ready, n_xn[0] * NT + b)
                    w = (b - a) * P
                    for c in range(KC):
                        for t in range(a, b):
                            ins = pe.transpose(ps[:, g, c * w + (t - a) * P:c * w + (t - a + 1) * P],
                                               xn[:, t, c * P:(c + 1) * P], idn[:])
                    ins.then_inc(xT_ps, 1)
                    if gate_w is not None and g:
                        logits(g - 1, gate_w)
                if gate_w is not None:
                    logits(len(TOK_GROUPS) - 1, gate_w)
                n_xn[0] += 1

            def xT_whole():
                pe.wait_ge(xT_ready, len(TOK_GROUPS) * n_xn[0])

            def attention(layer, w, wo, w_in, wo_in):
                xT_make()
                pe.wait_ge(w_in, 16)
                xT_whole()
                for i, base in enumerate((D, 0)):
                    for half in range(2):
                        for m in range(KC):
                            product(ps[:, 4 * i + 2 * half + m, 0:HALF],
                                    [(w[:, k, base + m * P:base + (m + 1) * P],
                                      xT[:, k, half * HALF:(half + 1) * HALF]) for k in range(KC)]).then_inc(qk_ps, 1)
                pe.wait_ge(qT_ready, 4 * layer + 4)
                if layer == 0:
                    pe.wait_ge(consts, 6)
                pe.wait_ge(ld["masks"], 48)
                for i in range(NPAIR + 4):
                    n = layer * NPAIR + i
                    if i < NPAIR:
                        if i >= 2:
                            pe.wait_ge(s_shifted, n - 1)
                        for m in range(KC):
                            if i == 0:
                                pe.wait_ge(kbd_dve, 2 * layer + m + 1)
                                pe.wait_ge(kbd_pool, 2 * layer + m + 1)
                            bank = 4 + 2 * (i % 2) + m
                            if layer == 1:
                                pe.matmul(ps[:, bank, 0:HM * T], spreadm[:], bandm[:], start=True, stop=False,
                                          skip_group_check=True)
                            for j in range(2):
                                b = 2 * i + j
                                ins = pe.matmul(ps[j * SLOT:(j + 1) * SLOT, bank, 0:HM * T],
                                                qT[:, m, b * T:b * T + SLOT], kbd[:, m, :, b * T:(b + 1) * T],
                                                start=(layer == 0), stop=True, skip_group_check=True)
                        ins.then_inc(s_ps, 1)
                    if i == 1:
                        for g in range(4):
                            for b in range(4 * g, 4 * g + 4):
                                for par in range(2):
                                    c0 = 2 * D + par * P
                                    ins = product(ps[par * SLOT:(par + 1) * SLOT, g, (b % 4) * P:(b % 4 + 1) * P],
                                                  [(xT[:, k, b * T:b * T + SLOT], w[:, k, c0:c0 + P])
                                                   for k in range(KC)])
                            ins.then_inc(v_ps, 1)
                    if 3 <= i < NPAIR + 3:
                        p = i - 3
                        pe.wait_ge(pn, n - 3 + 1)
                        if p == 0:
                            pe.wait_ge(vbd_ready, 8 * layer + 8)
                        else:
                            pe.wait_ge(pT_ready, n - 3)
                        for c in range(HM):
                            ins = pe.transpose(ps[:, c // 4, (c % 4) * P:(c % 4 + 1) * P],
                                               pe_[:, p % 4, 2 * c:2 * c + 2, :].rearrange("p h s -> p (h s)"), idn[:])
                        ins.then_inc(pT_ps, 1)
                    if i >= 4:
                        p = i - 4
                        pe.wait_ge(pT_ready, n - 4 + 1)
                        if p >= 2:
                            pe.wait_ge(oT_ready, n - 4 - 1)
                        for j in range(2):
                            for c in range(HM):
                                q = slice(32 * (c % 4), 32 * (c % 4) + 32)
                                o = (c // 4) * 2 * T + j * T
                                ins = pe.matmul(ps[q, 2 + p % 2, o:o + T], vbd[:, 2 * p + j, c, :],
                                                pT[:, p % 2, c, j, :], start=True, stop=True, skip_group_check=True,
                                                tile_position=(0, 32 * (c % 4)))
                        ins.then_inc(o_ps, 1)
                pe.wait_ge(wo_in, 16)
                for t in range(NT):
                    pairs = min(NPAIR, ceil((t + 1) * P / (2 * T)))
                    if t == NT - 1:
                        pairs = NPAIR
                    pe.wait_ge(oT_ready, layer * NPAIR + pairs)
                    product(ps[:, Z_BANKS[t], 0:D],
                            [(oT[:, k, t * P:(t + 1) * P], wo[:, k, :]) for k in range(KC)]).then_inc(proj_ps, 1)

            attention(0, wqkv0, wo0, ld["wqkv0"], ld["wo0"])

            xT_make(gatew)

            def hidden(n):
                pe.wait_ge(w1h_ready, n + 1)
                pe.wait_ge(w1l_ready, n + 1)
                for m in range(KC):
                    if n:
                        pe.wait_ge(relu_ready, 2 * n - 1 + m)
                    else:
                        pe.wait_ge(xl_ready, len(TOK_GROUPS))
                    for half in range(2):
                        cs = slice(half * HALF, (half + 1) * HALF)
                        ins = product(ps[:, 2 * m + half, 0:HALF],
                                      [x for k in range(KC) for x in split_terms(
                                          (w1h[:, n % 2, k, m * P:(m + 1) * P], w1l[:, n % 2, k, m * P:(m + 1) * P]),
                                          (xh[:, k, cs], xl[:, k, cs]))])
                    ins.then_inc(hid_ps, 1)

            def outputs(n):
                pe.wait_ge(w2h_ready, n + 1)
                pe.wait_ge(w2l_ready, n + 1)
                pe.wait_ge(hl_ready, 2 * n + 2)
                for k, tiles in enumerate(Y_BANKS):
                    if n:
                        pe.wait_ge(y_used, 3 * (n - 1) + k + 1)
                    for t in tiles:
                        m = min(P, N - t * P)
                        ts = slice(t * P, t * P + m)
                        ins = product(ps[0:m, 5 + k, (t % 2) * D:(t % 2 + 1) * D],
                                      [x for c in range(KC) for x in split_terms(
                                          (hh[:, n % 2, c, ts], hl[:, n % 2, c, ts]),
                                          (w2h[:, n % 2, c, :], w2l[:, n % 2, c, :]))])
                    ins.then_inc(y_ps, 1)

            hidden(0)
            for n in range(E + 1):
                if n < E:
                    hidden(n + 1)
                outputs(n)

            attention(1, wat1, wat1[:, :, 3 * D:4 * D], ld["wat1"], ld["wat1"])

            xT_make(wgw)
            pe.wait_ge(oh_ready, 1)
            for t in range(NT):
                ins = product(ps[:, 5, t * E:(t + 1) * E],
                              [(upperm[:, 1, :], ohb[:, s, :]) for s in range(t)] + [(upperm[:, 0, :], ohb[:, t, :])])
            ins.then_inc(cum_ps, 1)
            pe.wait_ge(tl_ready, 1)
            for t in range(NT):
                pe.wait_ge(sel_ready, t + 1)
                for j in range(4):
                    s, k = j // 2, j % 2
                    for part_ in (th, tl):
                        ins = pe.matmul(ps[:, j, 0:half_slots], part_[:, t, k * P:(k + 1) * P],
                                        sel[:, t, s * half_slots:(s + 1) * half_slots],
                                        start=(t == 0 and part_ is th), stop=(t == NT - 1 and part_ is tl),
                                        skip_group_check=True)
                    if t == NT - 1:
                        ins.then_inc(xg_ps, 1)
            for t in range(NT):
                pe.wait_ge(dg_ready, t + 1)
                ins = pe.matmul(ps[0:CAP, 6 + t // 4, (t % 4) * P:(t % 4 + 1) * P], onesm[:, 0:CAP], dg[:, t, :],
                                start=True, stop=True, skip_group_check=True)
                if t >= 3:
                    ins.then_inc(slotb_ps, 1)

            def up(e):
                pe.wait_ge(ld_f1[e % RING], 16 * (e // RING + 1))
                pe.wait_ge(xg_ready, 2 if e == 0 else 4)
                if e >= 2:
                    pe.wait_ge(gelu_ready, 2 * (e - 1))
                for q in range(2):
                    for f in range(4 * q, 4 * q + 4):
                        ins = product(ps[:, 2 * (e % 2) + q, (f % 4) * CAP:(f % 4 + 1) * CAP],
                                      [(fw1[:, e % RING, k, f * P:(f + 1) * P], xg[:, k, e * CAP:(e + 1) * CAP])
                                       for k in range(KC)])
                    ins.then_inc(fh_ps, 1)

            def down(e):
                pe.wait_ge(ld_f2[e % RING], 16 * (e // RING + 1))
                pe.wait_ge(gelu_ready, 2 * e + 2)
                if e >= 2:
                    pe.wait_ge(yt_ready, e - 1)
                product(ps[0:CAP, 4 + e % 2, 0:D],
                        [(hT[:, e % 2, f, :], fw2[:, e % RING, f, :]) for f in range(FC)]).then_inc(fy_ps, 1)

            up(0)
            for e in range(E):
                if e + 1 < E:
                    up(e + 1)
                down(e)
            pe.wait_ge(selT_ready, E)
            pe.wait_ge(yl_ready, E)
            for t in range(NT):
                product(ps[:, (6, 7, 0, 1, 2)[t], 0:D],
                        [(selT[:, e, t * P:(t + 1) * P], part_[:, e, :]) for e in range(E) for part_ in (yh, yl)])\
                    .then_inc(comb_ps, 1)


def layouts(x, cls_tok, L0_tok_ln1_g, L0_tok_ln1_b, L0_tok_W_proj, L0_tok_b_proj, L0_tok_ln2_g, L0_tok_ln2_b,
            L0_tok_cls_token, L0_tok_pos_emb, L0_attn_ln_gamma, L0_attn_ln_beta, L0_attn_W_qkv, L0_attn_b_qkv,
            L0_attn_W_proj, L0_attn_b_proj, L0_ffn_gate_w, L0_ffn_lb_bias, L0_ffn_w1, L0_ffn_w2, L0_ffn_cfc,
            L0_ffn_cproj, L1_attn_Wq, L1_attn_bq, L1_attn_Wk, L1_attn_bk, L1_attn_Wv, L1_attn_bv, L1_attn_Wo,
            L1_attn_bo, L1_ffn_wg, L1_ffn_W1, L1_ffn_b1, L1_ffn_W2, L1_ffn_b2):
    import numpy as np

    f32 = np.float32
    side = x.shape[2] // 6

    def by_token(a):
        a = np.concatenate([a.reshape(N, -1), np.zeros((NP - N, a.shape[-1]), f32)])
        return np.ascontiguousarray(a.reshape(NT, P, -1).transpose(1, 0, 2))

    def by_row(w):
        return np.ascontiguousarray(w.reshape(-1, P, w.shape[-1]).transpose(1, 0, 2))

    def by_col(a):
        return a.reshape(-1, P).T

    def odd_even(w):
        return w.reshape(w.shape[0], H // 2, 2, DH).transpose(0, 2, 1, 3).reshape(w.shape[0], D)

    pt = x.reshape(B, 3, 6, side, 6, side).transpose(0, 2, 4, 3, 5, 1).reshape(B, 36, PD)
    patches = by_token(np.concatenate([np.zeros((B, 2, PD), f32), pt], axis=1))
    wide = np.zeros((B, T, D), f32)
    scale_tok = wide.copy()
    scale_tok[:, 2:] = L0_tok_ln2_g
    shift_a = wide.copy()
    shift_a[:, 0] = cls_tok[0, 0]
    shift_a[:, 1:] = L0_tok_pos_emb[0]
    shift_b = wide.copy()
    shift_b[:, 1] = L0_tok_cls_token[0, 0]
    shift_b[:, 2:] = L0_tok_ln2_b
    w_qkv = by_row(np.concatenate([L0_attn_W_qkv[:, :2 * D], odd_even(L0_attn_W_qkv[:, 2 * D:])], axis=1))
    w_moe = np.stack([np.concatenate([by_row(a.T), by_row(b.T)], axis=1)
                      for a, b in [*zip(L0_ffn_w1, L0_ffn_w2), (L0_ffn_cfc, L0_ffn_cproj)]], axis=1)
    w_attn1 = by_row(np.concatenate([L1_attn_Wq.T, L1_attn_Wk.T, odd_even(L1_attn_Wv.T), L1_attn_Wo.T], axis=1))
    w1 = np.ascontiguousarray(L1_ffn_W1.reshape(E, KC, P, FF).transpose(2, 0, 1, 3))
    w2 = np.ascontiguousarray(L1_ffn_W2.reshape(E, FC, P, D).transpose(2, 0, 1, 3))
    bq0, bk0, bv0 = L0_attn_b_qkv.reshape(3, D)
    part = np.arange(P)
    head = (part[:, None] // DH == np.arange(HM)).astype(f32)
    slot0 = (part[:, None] + CAP * np.arange(E)).astype(f32)
    cols = np.concatenate([by_col(a) for a in (L0_tok_ln1_g, L0_tok_ln1_b, L0_attn_ln_gamma, L0_attn_ln_beta,
                                               bq0, bk0, bv0, L1_attn_bq, L1_attn_bk, L1_attn_bv, L1_ffn_b1)]
                          + [head, slot0], axis=1)
    rows = np.concatenate([L0_tok_b_proj, L0_attn_b_proj, L1_attn_bo, L0_ffn_lb_bias, np.arange(E).astype(f32)])
    near = np.abs(np.arange(T)[:, None] - np.arange(T)[None, :]) <= 3
    band = np.tile(np.where(near, 0.0, -1e30).astype(f32), (1, HM))
    spread = np.zeros((T, 2, SLOT), f32)
    spread[:, :, :T] = np.eye(T, dtype=f32)[:, None, :]
    upper = np.stack([np.triu(np.ones((P, P), f32)), np.ones((P, P), f32)], axis=1)
    bf = np.dtype("bfloat16")
    return {
        "patches": patches, "scale_tok": by_token(scale_tok), "shift_a": by_token(shift_a),
        "shift_b": by_token(shift_b), "w_patch": by_row(L0_tok_W_proj), "w_qkv": w_qkv,
        "w_out": by_row(L0_attn_W_proj), "gate": by_row(L0_ffn_gate_w.T), "w_moe": np.ascontiguousarray(w_moe),
        "w_attn1": w_attn1, "wg": by_row(L1_ffn_wg), "w1": w1, "w2": w2, "cols": np.ascontiguousarray(cols),
        "rows": np.ascontiguousarray(np.broadcast_to(rows, (P, NROWS))),
        "b2_rows": np.ascontiguousarray(np.broadcast_to(L1_ffn_b2, (P, E, D))),
        "iota_slots": np.ascontiguousarray(np.broadcast_to(np.arange(E * CAP, dtype=f32), (P, E * CAP))),
        "ident": np.eye(P, dtype=f32), "band": band.astype(bf), "spread": spread.reshape(T, P).astype(bf),
        "upper": upper.astype(bf),
    }


def kernel(**inputs):
    import numpy as np
    import concourse.bacc as bacc
    from concourse import mybir as mb
    from concourse.bass_utils import run_bass_kernel_spmd as run

    arrays = {f"in_{name}": a for name, a in layouts(**{k: np.asarray(v) for k, v in inputs.items()}).items()}
    nc = bacc.Bacc("TRN2", target_bir_lowering=False, num_devices=1)
    args = [nc.dram_tensor(name, a.shape, mb.dt.from_np(a.dtype), kind="ExternalInput").ap()
            for name, a in arrays.items()]
    result = nc.dram_tensor("out_0", (N, D), mb.dt.float32, kind="ExternalOutput").ap()
    vit_kernel(nc, *args, result)
    r = run(nc, [arrays], core_ids=[0])
    return r.results[0]["out_0"].reshape(B, T, D)
```

```python
import concourse.bass as bass
from concourse import mybir
from contextlib import ExitStack
from math import ceil

ALU = mybir.AluOpType
ACT = mybir.ActivationFunctionType
AX_X = mybir.AxisListType.X
F32 = mybir.dt.float32
F32R = mybir.dt.float32r
BF16 = mybir.dt.bfloat16
U32 = mybir.dt.uint32


P = 128
B = 16
T = 38
N = B * T
NT = 5
NP = NT * P
HALF = N // 2
D = 256
KC = D // P
PD = 768
PC = PD // P
H = 16
DH = D // H
HM = P // DH
NPAIR = B // 2
SLOT = 64
E = 8
CAP = int(N / E * 1.25) + 1
FF = 1024
FC = FF // P
SCALE = float(DH) ** -0.5
EPS = 1e-5
TOK_GROUPS = ((0, 2), (2, 4), (4, 5))
WARM = {"start": 12, "patches": 0, "groups": (14, 5), "halves": (4, 4), "dense": 2, "gate": 2, "top1": 8, "slots": 8}
RING = 3

COLS = {}
_at = 0
for _name, _n in (("ln1_g", PC), ("ln1_b", PC), ("lng", KC), ("lnb", KC),
                  ("bq0", KC), ("bk0", KC), ("bv0", KC), ("bq1", KC), ("bk1", KC), ("bv1", KC),
                  ("b1", E * FC), ("head", HM), ("slot0", E)):
    COLS[_name] = (_at, _at + _n)
    _at += _n
NCOLS = _at
ROWS = {}
_at = 0
for _name, _n in (("bo0", D), ("bo1", D), ("lb", E), ("iota", E)):
    ROWS[_name] = (_at, _at + _n)
    _at += _n
NROWS = _at


def vit_kernel(nc, patches, scale_tok, shift_a, shift_b, w_patch, w_qkv, w_out, gate, w_moe, w_attn1, wg, w1, w2,
               cols, rows, b_patch, b2_rows, iota_slots, ident, band, spread, upper, out):
    with ExitStack() as ctx:
        def sb(name, shape, dt=F32):
            return ctx.enter_context(nc.sbuf_tensor(name, shape, dt))

        def sem(name):
            return ctx.enter_context(nc.semaphore(name))

        def part(whole, at, shape, dt=F32):
            n = 1
            for x in shape:
                n *= x
            words = n // 2 if dt == BF16 else n
            ap = whole[:, at:at + words]
            if dt == BF16:
                ap = ap.bitcast(BF16)
            names = "abcd"[:len(shape)]
            spec = f"p ({' '.join(names)}) -> p {' '.join(names)}"
            return ap.rearrange(spec, **dict(zip(names, shape))), at + words

        ps = ctx.enter_context(nc.psum_tensor("ps", [P, 8, 512], F32))

        col = sb("col", [P, NCOLS])
        row = sb("row", [P, NROWS])
        bz = sb("bz", [1, D])
        idn = sb("idn", [P, P])
        bandm = sb("bandm", [T, HM * T], BF16)
        spreadm = sb("spreadm", [T, P], BF16)
        upperm = sb("upperm", [P, 2, P], BF16)
        onesm = sb("onesm", [P, P])
        neghalf = sb("neghalf", [P, NT])
        first_use = sb("first_use", [P, 2])
        wo0 = sb("wo0", [P, KC, D])
        gatew = sb("gatew", [P, KC, E])
        wgw = sb("wgw", [P, KC, E])
        weights = sb("weights", [P, RING * (KC * FF + FC * D)])
        wmoe, _ = part(weights, 0, [E + 1, 2 * KC, D])
        fw1, at = part(weights, 0, [RING, KC, FF])
        fw2, at = part(weights, at, [RING, FC, D])
        early = sb("early", [P, PC * D + KC * 3 * D])
        wz, at = part(early, 0, [PC, D])
        wqkv0, _ = part(early, at, [KC, 3 * D])
        b2r, at = part(early, 0, [E, D])
        iota, _ = part(early, at, [E * CAP])
        values = sb("values", [P, B * HM * 2 * DH])
        vbd, _ = part(values, 0, [B, HM, 2 * DH])
        xg, at = part(values, 0, [KC, E * CAP])
        hT, at = part(values, at, [2, FC, CAP])
        dg, at = part(values, at, [NT, P])
        zt = sb("zt", [P, NT, D])
        h = sb("h", [P, NT, D])
        hb = sb("hb", [P, NT, D])
        xn = sb("xn", [P, NT, D])
        xT = sb("xT", [P, KC, NP])
        st = sb("st", [P, NT, 2, 6])
        mv = sb("mv", [P, NT, 2])
        ve = sb("ve", [P, NT])
        rstd = sb("rstd", [P, NT])
        nb = sb("nb", [P, NT])
        sd = sb("sd", [P, 2, H, T])
        mx = sb("mx", [P, 2, H])
        rs = sb("rs", [P, 2, H])
        ri = sb("ri", [P, 2, H])
        pT = sb("pT", [P, 2, HM, 2, T])
        lg = sb("lg", [P, NT, E])
        lgb = sb("lgb", [P, NT, E])
        m8 = sb("m8", [P, NT, 8])
        i8 = sb("i8", [P, NT, 8], U32)
        i8f = sb("i8f", [P, NT, 2])
        ga = sb("ga", [P, NT, E])
        gb = sb("gb", [P, NT, E])
        sg = sb("sg", [P, NT, E])
        we = sb("we", [P, NT, E])
        s5 = sb("s5", [P, 4, NT])
        ohb = sb("ohb", [P, NT, E], BF16)
        slotb = sb("slotb", [CAP, NP])
        rl = sd[:].rearrange("p a h t -> p (a h t)").rearrange("p (m h t) -> p m h t", m=2, h=2)
        hsq = pT[:].rearrange("p a h b t -> p (a h b t)").rearrange("p (m h t) -> p m h t", m=2, h=2)
        yt = hb
        res = zt

        def staged(stage, dt, *arrays, parts=P):
            return [stage.enter_context(nc.sbuf_tensor(n, [parts, *x], dt)) for n, x in arrays]

        with ExitStack() as stage:
            wat1, qT, kT, oT, pe_ = staged(stage, F32, ("wat1", (KC, 4 * D)), ("qT", (KC, NP)), ("kT", (KC, N)),
                                           ("oT", (KC, NP)), ("pe_", (4, H, SLOT)))
            with ExitStack() as inner:
                tok, ztr, gsc, sha, shb = staged(inner, F32, ("tok", (NT, PD)), ("ztr", (PC, NP)), ("gsc", (NT, D)),
                                                 ("sha", (NT, D)), ("shb", (NT, D)))
            with ExitStack() as inner:
                kbd, = staged(inner, F32, ("kbd", (KC, HM, N)))
            with ExitStack() as inner:
                xh, xl, w1h, w1l, w2h, w2l, hh, hl = staged(
                    inner, F32R, ("xh", (KC, NP)), ("xl", (KC, NP)), ("w1h", (2, KC, D)), ("w1l", (2, KC, D)),
                    ("w2h", (2, KC, D)), ("w2l", (2, KC, D)), ("hh", (2, KC, N)), ("hl", (2, KC, N)))
        with ExitStack() as stage:
            f2h, f2l, fhh, fhl = staged(stage, F32R, ("f2h", (2, FC, D)), ("f2l", (2, FC, D)),
                                        ("fhh", (FC, CAP)), ("fhl", (FC, CAP)))
            selT, = staged(stage, F32R, ("selT", (E, NP)), parts=CAP)
            with ExitStack() as inner:
                th, tl, sel = staged(inner, F32R, ("th", (NT, D)), ("tl", (NT, D)), ("sel", (NT, E * CAP)))
            with ExitStack() as inner:
                yh, yl = staged(inner, F32R, ("yh", (E, D)), ("yl", (E, D)), parts=CAP)

        def c_(name, i=0, n=1):
            return col[:, COLS[name][0] + i:COLS[name][0] + i + n]

        def r_(name):
            return row[:, ROWS[name][0]:ROWS[name][1]]

        ld_tok = [sem(f"ld_tok{t}") for t in range(NT)]
        ld = {n: sem("ld_" + n) for n in ("col", "bz", "row", "b2", "iota", "idn", "masks", "wz", "gsc", "shift",
                                          "wqkv0", "wo0", "gate", "wat1")}
        ld_moe = [sem(f"ld_moe{e}") for e in range(E + 1)]
        ld_f1 = [sem(f"ld_f1_{r}") for r in range(RING)]
        ld_f2 = [sem(f"ld_f2_{r}") for r in range(RING)]
        consts = sem("consts")
        dve = sem("dve")
        var_ready = sem("var_ready")
        rstd_ready = sem("rstd_ready")
        nb_ready = sem("nb_ready")
        pn_ready = sem("pn_ready")
        ztr_ps = sem("ztr_ps")
        ztr_ready = sem("ztr_ready")
        z_ps = sem("z_ps")
        shift_ready = sem("shift_ready")
        h_ready = sem("h_ready")
        hb_ready = sem("hb_ready")
        xn_ready = sem("xn_ready")
        xT_ps = sem("xT_ps")
        xT_ready = sem("xT_ready")
        xh_ready = sem("xh_ready")
        xl_ready = sem("xl_ready")
        qk_ps = sem("qk_ps")
        kT_ready = sem("kT_ready")
        qT_ready = sem("qT_ready")
        kbd_dve = sem("kbd_dve")
        kbd_pool = sem("kbd_pool")
        v_ps = sem("v_ps")
        vbd_ready = sem("vbd_ready")
        s_ps = sem("s_ps")
        s_shifted = sem("s_shifted")
        exp_ready = sem("exp_ready")
        rs_ready = sem("rs_ready")
        pn = sem("pn")
        pT_ps = sem("pT_ps")
        pT_ready = sem("pT_ready")
        o_ps = sem("o_ps")
        oT_ready = sem("oT_ready")
        proj_ps = sem("proj_ps")
        lg_ps = sem("lg_ps")
        lg_ready = sem("lg_ready")
        ex_ready = sem("ex_ready")
        hid_ps = sem("hid_ps")
        relu_ready = sem("relu_ready")
        hh_ready = sem("hh_ready")
        hl_ready = sem("hl_ready")
        y_ps = sem("y_ps")
        y_used = sem("y_used")
        w1h_ready = sem("w1h_ready")
        w1l_ready = sem("w1l_ready")
        w2h_ready = sem("w2h_ready")
        w2l_ready = sem("w2l_ready")
        th_ready = sem("th_ready")
        tl_ready = sem("tl_ready")
        oh_ready = sem("oh_ready")
        cum_ps = sem("cum_ps")
        dg_ready = sem("dg_ready")
        slotb_ps = sem("slotb_ps")
        slotb_ready = sem("slotb_ready")
        sel_ready = sem("sel_ready")
        selT_ready = sem("selT_ready")
        xg_ps = sem("xg_ps")
        xg_ready = sem("xg_ready")
        fh_ps = sem("fh_ps")
        gelu_ready = sem("gelu_ready")
        fhh_ready = sem("fhh_ready")
        fhl_ready = sem("fhl_ready")
        f2h_ready = sem("f2h_ready")
        f2l_ready = sem("f2l_ready")
        fy_ps = sem("fy_ps")
        yt_ready = sem("yt_ready")
        yh_ready = sem("yh_ready")
        yl_ready = sem("yl_ready")
        comb_ps = sem("comb_ps")
        res_ready = sem("res_ready")
        stored = sem("stored")

        Y_BANKS = ((0, 1), (2, 3), (4,))
        XT_BANKS = (0, 1, 3)
        Z_BANKS = (4, 5, 6, 7, 3)
        half_slots = E * CAP // 2

        def expert(n):
            return (n - 1) % (E + 1)

        block = ctx.enter_context(nc.Block())

        @block.sync
        def _(sp):
            def load(dst, src, s):
                sp.dma_start(dst, src).then_inc(s, 16)

            load(tok[:, 0, :], patches[:, 0, :], ld_tok[0])
            load(bz[:], b_patch, ld["bz"])
            load(tok[:, 1, :], patches[:, 1, :], ld_tok[1])
            load(idn[:], ident, ld["idn"])
            load(col[:], cols, ld["col"])
            load(wz[:], w_patch, ld["wz"])
            for t in range(2, NT):
                load(tok[:, t, :], patches[:, t, :], ld_tok[t])
            load(row[:], rows, ld["row"])
            load(gsc[:], scale_tok, ld["gsc"])
            load(sha[:], shift_a, ld["shift"])
            load(shb[:], shift_b, ld["shift"])
            load(wqkv0[:], w_qkv, ld["wqkv0"])
            load(bandm[:], band, ld["masks"])
            load(spreadm[:], spread, ld["masks"])
            load(upperm[:], upper, ld["masks"])
            load(wo0[:], w_out, ld["wo0"])
            load(gatew[:], gate, ld["gate"])
            load(wgw[:], wg, ld["gate"])
            for n in range(E + 1):
                load(wmoe[:, expert(n)], w_moe[:, expert(n)], ld_moe[expert(n)])
            load(wat1[:], w_attn1, ld["wat1"])
            sp.wait_ge(w1l_ready, E + 1)
            sp.wait_ge(w2l_ready, E + 1)
            load(iota[:], iota_slots, ld["iota"])
            load(b2r[:], b2_rows, ld["b2"])
            for e in range(E):
                if e >= RING:
                    sp.wait_ge(fh_ps, 2 * (e - RING + 1))
                load(fw1[:, e % RING], w1[:, e], ld_f1[e % RING])
                if e >= RING:
                    sp.wait_ge(f2l_ready, e - RING + 1)
                load(fw2[:, e % RING], w2[:, e], ld_f2[e % RING])
            for t in range(NT):
                n = min(P, N - t * P)
                sp.wait_ge(res_ready, t + 1)
                sp.dma_start(out[t * P:t * P + n, :], res[0:n, t, :]).then_inc(stored, 16)
            sp.wait_ge(stored, 16 * NT)

        @block.gpsimd
        def _(gp):
            gp.memset(neghalf[:], -0.5).then_inc(consts, 1)
            gp.memset(onesm[:], 1.0).then_inc(consts, 1)
            gp.memset(vbd[:], 0.0).then_inc(consts, 1)
            gp.wait_ge(consts, 1)
            n_rstd = [0]

            def rstd_step(t):
                n_rstd[0] += 1
                gp.wait_ge(var_ready, n_rstd[0])
                gp.tensor_tensor(rstd[:, t:t + 1], ve[:, t:t + 1], neghalf[:, t:t + 1], ALU.pow)\
                  .then_inc(rstd_ready, 1)

            def nb_step(t):
                gp.wait_ge(rstd_ready, n_rstd[0])
                gp.tensor_scalar(nb[:, t:t + 1], mv[:, t, 0:1], rstd[:, t:t + 1], -1.0, ALU.mult, ALU.mult)\
                  .then_inc(nb_ready, 1)

            for t in range(NT):
                rstd_step(t)
            gp.memset(qT[:, :, N:NP], 0.0).then_inc(consts, 1)
            gp.memset(oT[:, :, N:NP], 0.0).then_inc(consts, 1)
            gp.memset(pe_[:, :, :, T:SLOT], 0.0).then_inc(consts, 1)
            gp.wait_ge(ld["shift"], 32)

            def shift(t):
                gp.tensor_tensor(shb[:, t, :], sha[:, t, :], shb[:, t, :], ALU.add).then_inc(shift_ready, 1)

            shift(0)
            shift(1)
            for step in range(NT + 1):
                for lag in (0, 1):
                    if 0 <= step - lag < NT:
                        rstd_step(step - lag)
                        if lag:
                            nb_step(step - lag)
                if step + 2 < NT:
                    shift(step + 2)

            def add_bias(name, n):
                gp.wait_ge(xn_ready, NT * n)
                for t in range(NT):
                    gp.tensor_tensor(hb[:, t, :], h[:, t, :], r_(name), ALU.add).then_inc(hb_ready, 1)

            def attention(layer):
                for n in range(4):
                    m, cs = n % 2, slice(n // 2 * HALF, (n // 2 + 1) * HALF)
                    gp.wait_ge(kT_ready, 4 * layer + n + 1)
                    for hh_ in range(HM // 2, HM):
                        ins = gp.tensor_scalar(kbd[:, m, hh_, cs], kT[:, m, cs], c_("head", hh_), 1.0,
                                               ALU.mult, ALU.mult)
                    ins.then_inc(kbd_pool, 1)
                for p in range(NPAIR):
                    gp.wait_ge(rs_ready, layer * NPAIR + p + 1)
                    w = pe_[:, p % 4, :, 0:T]
                    gp.tensor_tensor(w, w, ri[:, p % 2, :].unsqueeze(2).broadcast_to([P, H, T]), ALU.mult)\
                      .then_inc(pn, 1)

            def low_part(n, k, dst, high_, high_ready, ready):
                gp.wait_ge(high_ready, n + 1)
                gp.tensor_tensor(dst[:, n % 2], wmoe[:, expert(n), k * KC:(k + 1) * KC, :],
                                 high_[:, n % 2].bitcast(F32), ALU.subtract).then_inc(ready, 1)

            add_bias("bo0", 1)
            attention(0)
            low_part(0, 0, w1l, w1h, w1h_ready, w1l_ready)
            for t in range(NT):
                rstd_step(t)
            low_part(1, 0, w1l, w1h, w1h_ready, w1l_ready)
            low_part(0, 1, w2l, w2h, w2h_ready, w2l_ready)
            for n in range(E + 1):
                if n + 2 <= E:
                    low_part(n + 2, 0, w1l, w1h, w1h_ready, w1l_ready)
                if n + 1 <= E:
                    low_part(n + 1, 1, w2l, w2h, w2h_ready, w2l_ready)
            for t in range(NT):
                rstd_step(t)
                nb_step(t)
            add_bias("bo1", 3)
            attention(1)
            for t in range(NT):
                rstd_step(t)
            gp.wait_ge(th_ready, 1)
            gp.tensor_tensor(tl[:], xn[:], th[:].bitcast(F32), ALU.subtract).then_inc(tl_ready, 1)

        @block.scalar
        def _(sc):
            sc.wait_ge(consts, 1)
            sc.activation(first_use[:, 0:1], neghalf[:, 0:1], ACT.Exp)
            sc.wait_ge(ld["col"], 16)
            for g, (a, b) in enumerate(TOK_GROUPS):
                for i in range(PC // 2):
                    j = g * (PC // 2) + i
                    sc.wait_ge(ztr_ps, j + 1)
                    for c in (2 * i, 2 * i + 1):
                        w = (b - a) * P
                        ins = sc.activation(ztr[:, c, a * P:b * P], ps[:, j % 3, (c % 2) * w:(c % 2 + 1) * w],
                                            ACT.Identity, scale=c_("ln1_g", c), bias=c_("ln1_b", c))
                    ins.then_inc(ztr_ready, 1)

            n_xT = [0]

            def xT_evict(kind, groups=range(len(TOK_GROUPS))):
                for g in groups:
                    a, b = TOK_GROUPS[g]
                    n_xT[0] += 1
                    sc.wait_ge(xT_ps, n_xT[0])
                    src = ps[:, XT_BANKS[g], 0:KC * (b - a) * P].rearrange("p (c n) -> p c n", c=KC)
                    if kind == "affine":
                        for c in range(KC):
                            ins = sc.activation(xT[:, c, a * P:b * P], src[:, c, :], ACT.Identity,
                                                scale=c_("lng", c), bias=c_("lnb", c))
                    else:
                        if kind == "split":
                            sc.activation(xh[:, :, a * P:b * P], src, ACT.Copy).then_inc(xh_ready, 1)
                        ins = sc.activation(xT[:, :, a * P:b * P], src, ACT.Copy)
                    ins.then_inc(xT_ready, 1)

            def high_part(n, k, dst, used, ready):
                if used is not None:
                    sc.wait_ge(*used)
                sc.wait_ge(ld_moe[expert(n)], 16)
                sc.activation(dst[:, n % 2], wmoe[:, expert(n), k * KC:(k + 1) * KC, :], ACT.Copy).then_inc(ready, 1)

            def attention(layer):
                kind = "whole" if layer else "affine"
                for half in range(2):
                    if half == 0:
                        for t in range(NT):
                            if t == TOK_GROUPS[2][0]:
                                xT_evict(kind, range(2))
                            sc.wait_ge(nb_ready, layer * NT + t + 1)
                            sc.activation(xn[:, t, :], h[:, t, :], ACT.Identity, scale=rstd[:, t:t + 1],
                                          bias=nb[:, t:t + 1]).then_inc(xn_ready, 1)
                    for i, (dst, name, ready) in enumerate(((kT, "bk", kT_ready), (qT, "bq", qT_ready))):
                        if half == 0 and i == 1:
                            xT_evict(kind, [2])
                        for m in range(KC):
                            sc.wait_ge(qk_ps, 8 * layer + 4 * half + 2 * i + m + 1)
                            sc.activation(dst[:, m, half * HALF:(half + 1) * HALF],
                                          ps[:, 4 * i + 2 * half + m, 0:HALF], ACT.Identity,
                                          bias=c_(f"{name}{layer}", m)).then_inc(ready, 1)

                def values_evict(g):
                    sc.wait_ge(v_ps, 4 * layer + g + 1)
                    for par in range(2):
                        q = slice(par * SLOT, (par + 1) * SLOT)
                        src = ps[q, g, :].rearrange("p (b h d) -> p b h d", b=4, h=HM)
                        sc.copy(vbd[q, 4 * g:4 * g + 4, :, par * DH:(par + 1) * DH], src).then_inc(vbd_ready, 1)

                values_evict(0)
                for i in range(NPAIR + 4):
                    n = layer * NPAIR + i
                    if i == 3:
                        values_evict(3)
                    if 3 <= i < NPAIR + 3:
                        sc.wait_ge(pT_ps, n - 3 + 1)
                        if i - 3 >= 2:
                            sc.wait_ge(o_ps, n - 3 - 1)
                        src = ps[:, 0:2, :].rearrange("p k (h b s) -> p (k h) b s", h=4, b=2)
                        sc.copy(pT[:, (i - 3) % 2], src[:, :, :, 0:T]).then_inc(pT_ready, 1)
                    if i < NPAIR:
                        sc.wait_ge(s_shifted, n + 1)
                        if i >= 4:
                            sc.wait_ge(pT_ps, n - 4 + 1)
                        elif layer == 0:
                            sc.wait_ge(consts, 6)
                        sc.activation(pe_[:, i % 4, :, 0:T], sd[:, i % 2], ACT.Exp, scale=SCALE)\
                          .then_inc(exp_ready, 1)
                    if i in (1, 2):
                        values_evict(i)
                    if i >= 4:
                        p = i - 4
                        sc.wait_ge(o_ps, n - 4 + 1)
                        for m in range(KC):
                            ins = sc.activation(oT[:, m, p * 2 * T:(p + 1) * 2 * T],
                                                ps[:, 2 + p % 2, m * 2 * T:(m + 1) * 2 * T], ACT.Identity,
                                                bias=c_(f"bv{layer}", m))
                        ins.then_inc(oT_ready, 1)
                    if layer == 0 and i >= NPAIR:
                        if i < NPAIR + 2:
                            high_part(i - NPAIR, 0, w1h, None, w1h_ready)
                        elif i == NPAIR + 2:
                            high_part(0, 1, w2h, None, w2h_ready)

            attention(0)
            xT_evict("split")
            for n in range(E + 1):
                for m in range(KC):
                    sc.wait_ge(hid_ps, 2 * n + m + 1)
                    if n:
                        sc.wait_ge(hl_ready, 2 * n - 1 + m)
                    sc.activation(rl[:, m], ps[:, 2 * m:2 * m + 2, 0:HALF], ACT.Relu).then_inc(relu_ready, 1)
                    sc.wait_ge(relu_ready, 2 * n + m + 1)
                    if n >= 2:
                        sc.wait_ge(y_ps, 3 * (n - 1))
                    sc.activation(hh[:, n % 2, m, :].rearrange("p (a b) -> p a b", a=2), rl[:, m], ACT.Square)\
                      .then_inc(hh_ready, 1)
                if n == 0:
                    sc.wait_ge(lg_ready, 1)
                    sc.activation(sg[:], lg[:], ACT.Exp, scale=-1.0).then_inc(ex_ready, 1)
                if n + 2 <= E:
                    high_part(n + 2, 0, w1h, (hid_ps, 2 * n + 2), w1h_ready)
                if n + 1 <= E:
                    high_part(n + 1, 1, w2h, (y_ps, 3 * n) if n else None, w2h_ready)
            attention(1)
            xT_evict("whole")
            sc.wait_ge(xn_ready, 4 * NT)
            sc.activation(th[:], xn[:], ACT.Copy).then_inc(th_ready, 1)
            sc.wait_ge(lg_ready, 2)
            sc.activation(sg[:], ga[:], ACT.Exp).then_inc(ex_ready, 1)
            sc.activation(first_use[:, 1:2], neghalf[:, 0:1], ACT.Gelu)
            for j in range(4):
                sc.wait_ge(xg_ps, j + 1)
                s = j // 2
                sc.copy(xg[:, j % 2, s * half_slots:(s + 1) * half_slots], ps[:, j, 0:half_slots])\
                  .then_inc(xg_ready, 1)
            for i, (a, b) in enumerate(((0, 512), (512, NP))):
                sc.wait_ge(slotb_ps, i + 1)
                sc.copy(slotb[:, a:b], ps[0:CAP, 6 + i, 0:b - a]).then_inc(slotb_ready, 1)

            def high_y(e):
                sc.wait_ge(yt_ready, e + 1)
                sc.activation(yh[:, e, :], yt[0:CAP, e % 2, :], ACT.Copy).then_inc(yh_ready, 1)

            def high_w2(e):
                sc.wait_ge(ld_f2[e % RING], 16 * (e // RING + 1))
                sc.activation(f2h[:, e % 2], fw2[:, e % RING], ACT.Copy).then_inc(f2h_ready, 1)

            high_w2(0)
            for e in range(E):
                for q in range(2):
                    sc.wait_ge(fh_ps, 2 * e + q + 1)
                    if e >= 2 and q == 0:
                        sc.wait_ge(fhl_ready, e - 1)
                    for f in range(4 * q, 4 * q + 4):
                        ins = sc.activation(hT[:, e % 2, f, :], ps[:, 2 * (e % 2) + q, (f % 4) * CAP:(f % 4 + 1) * CAP],
                                            ACT.Gelu, bias=c_("b1", e * FC + f))
                    ins.then_inc(gelu_ready, 1)
                sc.wait_ge(gelu_ready, 2 * e + 2)
                if e:
                    sc.wait_ge(fy_ps, e)
                sc.activation(fhh[:], hT[:, e % 2], ACT.Copy).then_inc(fhh_ready, 1)
                if e:
                    high_y(e - 1)
                if e + 1 < E:
                    high_w2(e + 1)
            high_y(E - 1)

        @block.vector
        def _(v):
            own = [0]

            def mark(ins):
                own[0] += 1
                ins.then_inc(dve, 1)
                return own[0]

            def settle():
                v.wait_ge(dve, own[0])

            def done(ins):
                mark(ins)
                settle()

            n_rstd = [0]

            def next_rstd():
                n_rstd[0] += 1
                v.wait_ge(rstd_ready, n_rstd[0])

            def norms(t, src):
                return mark(v.bn_stats(st[:, t, 0, :], src))

            def mean_var(t, after):
                v.wait_ge(dve, after)
                return mark(v.bn_aggr(mv[:, t, :], st[:, t, 0, :]))

            def var_eps(t, after, twice=False):
                a, b = (1.0 + EPS, EPS * EPS) if twice else (1.0, EPS)
                v.wait_ge(dve, after)
                v.tensor_scalar(ve[:, t:t + 1], mv[:, t, 1:2], a, b, ALU.mult, ALU.add).then_inc(var_ready, 1)

            def norm_tiles(write, ahead=False):
                written = {}
                for step in range(NT + 2):
                    t, s_, c = step, step - 1, step - 2
                    if 0 <= s_ < NT:
                        v.wait_ge(dve, written[s_])
                        a = norms(s_, h[:, s_, :])
                    if ahead and t < NT:
                        written[t] = mark(write(t))
                    if 0 <= s_ < NT:
                        a = mean_var(s_, a)
                    if 0 <= c < NT and not ahead:
                        centre(xn, h, c).then_inc(xn_ready, 1)
                    if 0 <= s_ < NT:
                        var_eps(s_, a)
                    if not ahead and t < NT:
                        written[t] = mark(write(t))

            def centre(dst, src, t):
                next_rstd()
                return v.tensor_scalar(dst[:, t, :], src[:, t, :], mv[:, t, 0:1], rstd[:, t:t + 1],
                                       ALU.subtract, ALU.mult)

            def patch_stats(t):
                v.wait_ge(ld_tok[t], 16)
                for k in range(2):
                    mark(v.bn_stats(st[:, t, k, :], tok[:, t, k * (PD // 2):(k + 1) * (PD // 2)]))
                settle()
                done(v.bn_aggr(mv[:, t, :], st[:, t].rearrange("p k s -> p (k s)")))
                v.tensor_scalar(ve[:, t:t + 1], mv[:, t, 1:2], EPS, None, ALU.add).then_inc(var_ready, 1)

            for tiles in TOK_GROUPS:
                for t in range(*tiles):
                    patch_stats(t)
                for t in range(*tiles):
                    centre(tok, tok, t).then_inc(pn_ready, 1)

            v.wait_ge(ld["gsc"], 16)
            for step in range(NT + 1):
                z, t = step, step - 1
                if t >= 0:
                    scaled = mark(v.scalar_tensor_tensor(out=zt[:, t, :], in0=ps[:, Z_BANKS[t], 0:D],
                                                         scalar=mv[:, t, 0:1], in1=gsc[:, t, :],
                                                         op0=ALU.subtract, op1=ALU.mult))
                if z < NT:
                    v.wait_ge(z_ps, z + 1)
                    a = mean_var(z, norms(z, ps[:, Z_BANKS[z], 0:D]))
                if t >= 0:
                    v.wait_ge(rstd_ready, NT + max(1, 2 * t))
                    v.wait_ge(shift_ready, t + 1)
                    v.wait_ge(dve, scaled)
                    v.scalar_tensor_tensor(out=h[:, t, :], in0=zt[:, t, :], scalar=rstd[:, t:t + 1],
                                           in1=shb[:, t, :], op0=ALU.mult, op1=ALU.add).then_inc(h_ready, 1)
                if z < NT:
                    var_eps(z, a)
                if t >= 0:
                    v.wait_ge(h_ready, t + 1)
                    var_eps(t, mean_var(t, norms(t, h[:, t, :])), twice=True)
            n_rstd[0] += 2 * NT

            def attention(layer):
                for n in range(4):
                    m, cs = n % 2, slice(n // 2 * HALF, (n // 2 + 1) * HALF)
                    v.wait_ge(kT_ready, 4 * layer + n + 1)
                    for hh_ in range(HM // 2):
                        ins = v.tensor_scalar(kbd[:, m, hh_, cs], kT[:, m, cs], c_("head", hh_), None, ALU.mult)
                    ins.then_inc(kbd_dve, 1)
                for i in range(NPAIR + 1):
                    if i < NPAIR:
                        n = layer * NPAIR + i
                        v.wait_ge(s_ps, n + 1)
                        s = ps[:, 4 + 2 * (i % 2):6 + 2 * (i % 2), 0:HM * T].rearrange("p m (h k) -> p m h k", h=HM)
                        done(v.tensor_reduce(mx[:, i % 2, :].rearrange("p (m h) -> p m h", m=KC), s, AX_X, ALU.max))
                        if i >= 2:
                            v.wait_ge(exp_ready, n - 1)
                        mb = mx[:, i % 2, :].rearrange("p (m h) -> p m h", m=KC).unsqueeze(3)
                        v.tensor_tensor(sd[:, i % 2].rearrange("p (m h) k -> p m h k", m=KC), s,
                                        mb.broadcast_to([P, KC, HM, T]), ALU.subtract).then_inc(s_shifted, 1)
                    if i >= 1:
                        p = i - 1
                        v.wait_ge(exp_ready, layer * NPAIR + p + 1)
                        done(v.tensor_reduce(rs[:, p % 2, :], pe_[:, p % 4, :, 0:T], AX_X, ALU.add))
                        if p >= 2:
                            v.wait_ge(pn, layer * NPAIR + p - 1)
                        v.reciprocal(ri[:, p % 2, :], rs[:, p % 2, :]).then_inc(rs_ready, 1)
                def write(t):
                    v.wait_ge(proj_ps, layer * NT + t + 1)
                    v.wait_ge(hb_ready, layer * NT + t + 1)
                    return v.tensor_tensor(h[:, t, :], ps[:, Z_BANKS[t], 0:D], hb[:, t, :], ALU.add)

                norm_tiles(write)

            attention(0)

            for g, (a, b) in enumerate(TOK_GROUPS):
                v.wait_ge(xT_ready, len(TOK_GROUPS) + g + 1)
                v.tensor_tensor(xl[:, :, a * P:b * P], xT[:, :, a * P:b * P], xh[:, :, a * P:b * P].bitcast(F32),
                                ALU.subtract)\
                 .then_inc(xl_ready, 1)
            bc = [P, NT, E]
            it = r_("iota").unsqueeze(1).broadcast_to(bc)

            def choices(x):
                for t in range(NT):
                    mark(v.max(m8[:, t, :], x[:, t, :]))
                settle()
                for t in range(NT):
                    mark(v.max_index(i8[:, t, :], m8[:, t, :], x[:, t, :]))

            def gate_choices():
                v.wait_ge(lg_ready, 1)
                done(v.tensor_tensor(lgb[:], lg[:], r_("lb").unsqueeze(1).broadcast_to(bc), ALU.add))
                choices(lgb)
                settle()
                done(v.tensor_copy(i8f[:], i8[:, :, 0:2]))

            def gate_weights():
                mark(v.tensor_tensor(ga[:], it, i8f[:, :, 0:1].broadcast_to(bc), ALU.is_equal))
                done(v.tensor_tensor(gb[:], it, i8f[:, :, 1:2].broadcast_to(bc), ALU.is_equal))
                done(v.tensor_tensor(ga[:], ga[:], gb[:], ALU.add))
                v.wait_ge(ex_ready, 1)
                done(v.tensor_scalar(gb[:], sg[:], 1.0, None, ALU.add))
                done(v.reciprocal(sg[:], gb[:]))
                done(v.tensor_tensor(gb[:], sg[:], ga[:], ALU.mult))
                done(v.tensor_reduce(s5[:, 0, :], gb[:], AX_X, ALU.add))
                done(v.tensor_scalar(s5[:, 1, :], s5[:, 0, :], 1e-6, None, ALU.add))
                done(v.reciprocal(s5[:, 2, :], s5[:, 1, :]))
                done(v.tensor_tensor(we[:], gb[:], s5[:, 2, :].unsqueeze(2).broadcast_to(bc), ALU.mult))

            def squares(n):
                for m in range(KC):
                    v.wait_ge(relu_ready, 2 * n + m + 1)
                    done(v.tensor_tensor(hsq[:, m], rl[:, m], rl[:, m], ALU.mult))
                    v.wait_ge(hh_ready, 2 * n + m + 1)
                    if n >= 2 and m == 0:
                        v.wait_ge(y_ps, 3 * (n - 1))
                    v.tensor_tensor(hl[:, n % 2, m, :].rearrange("p (a b) -> p a b", a=2), hsq[:, m],
                                    hh[:, n % 2, m, :].rearrange("p (a b) -> p a b", a=2).bitcast(F32),
                                    ALU.subtract).then_inc(hl_ready, 1)

            def add_outputs(n, t):
                m = min(P, N - t * P)
                y = ps[0:m, 5 + t // 2, (t % 2) * D:(t % 2 + 1) * D]
                if n == 0:
                    return v.tensor_tensor(h[0:m, t, :], y, h[0:m, t, :], ALU.add)
                return v.scalar_tensor_tensor(out=h[0:m, t, :], in0=y, scalar=we[0:m, t, n - 1:n],
                                              in1=h[0:m, t, :], op0=ALU.mult, op1=ALU.add)

            def outputs_ready(n, k):
                v.wait_ge(y_ps, 3 * n + k + 1)
                if n:
                    v.wait_ge(y_used, 3 * (n - 1) + k + 1)

            def add_expert(n):
                for k, tiles in enumerate(Y_BANKS):
                    outputs_ready(n, k)
                    for t in tiles:
                        ins = add_outputs(n, t)
                    ins.then_inc(y_used, 1)

            def add_last(t):
                outputs_ready(E, t // 2)
                return add_outputs(E, t)

            v.wait_ge(lg_ps, 1)
            v.tensor_copy(lg[:], ps[:, 4, 0:NT * E].rearrange("p (t e) -> p t e", e=E)).then_inc(lg_ready, 1)
            squares(0)
            gate_choices()
            for n in range(E + 1):
                if n < E:
                    squares(n + 1)
                    add_expert(n)
                    if n == 0:
                        gate_weights()
            norm_tiles(add_last, ahead=True)
            n_rstd[0] += NT

            attention(1)

            v.wait_ge(lg_ps, 2)
            done(v.tensor_copy(lg[:], ps[:, 4, 0:NT * E].rearrange("p (t e) -> p t e", e=E)))
            choices(lg)
            settle()
            done(v.tensor_copy(i8f[:], i8[:, :, 0:2]))
            v.tensor_tensor(ohb[:], it, i8f[:, :, 0:1].broadcast_to(bc), ALU.is_equal).then_inc(oh_ready, 1)
            v.tensor_tensor(ga[:], lg[:], m8[:, :, 0:1].broadcast_to(bc), ALU.subtract).then_inc(lg_ready, 1)
            done(v.tensor_scalar(s5[:, 3, :], i8f[:, :, 0], float(CAP), -1.0, ALU.mult, ALU.add))
            v.wait_ge(cum_ps, 1)
            v.wait_ge(oh_ready, 1)
            done(v.tensor_tensor(gb[:], ps[:, 5, 0:NT * E].rearrange("p (t e) -> p t e", e=E), ohb[:], ALU.mult))
            done(v.tensor_reduce(s5[:, 2, :], gb[:], AX_X, ALU.add))
            mark(v.tensor_tensor(s5[:, 1, :], s5[:, 2, :], s5[:, 3, :], ALU.add))
            done(v.tensor_scalar(s5[:, 0, :], s5[:, 2, :], float(CAP), float(4 * E * CAP), ALU.is_gt, ALU.mult))
            done(v.tensor_tensor(s5[:, 2, :], s5[:, 1, :], s5[:, 0, :], ALU.add))
            v.wait_ge(ld["iota"], 16)
            for t in range(NT):
                v.tensor_scalar(sel[:, t, :], iota[:], s5[:, 2, t:t + 1], None, ALU.is_equal).then_inc(sel_ready, 1)
            for t in range(NT):
                v.tensor_scalar(dg[:, t, :], idn[:], s5[:, 2, t:t + 1], None, ALU.mult).then_inc(dg_ready, 1)
            v.wait_ge(ex_ready, 2)
            done(v.tensor_reduce(s5[:, 0, :], sg[:], AX_X, ALU.add))
            done(v.reciprocal(s5[:, 1, :], s5[:, 0, :]))

            def low_w2(e):
                v.wait_ge(f2h_ready, e + 1)
                v.tensor_tensor(f2l[:, e % 2], fw2[:, e % RING], f2h[:, e % 2].bitcast(F32), ALU.subtract)\
                 .then_inc(f2l_ready, 1)

            def outputs(e):
                v.wait_ge(fy_ps, e + 1)
                v.tensor_tensor(yt[0:CAP, e % 2, :], ps[0:CAP, 4 + e % 2, 0:D], b2r[0:CAP, e, :], ALU.add)\
                 .then_inc(yt_ready, 1)

            def low_y(e):
                v.wait_ge(yh_ready, e + 1)
                v.tensor_tensor(yl[:, e, :], yt[0:CAP, e % 2, :], yh[:, e, :].bitcast(F32), ALU.subtract)\
                 .then_inc(yl_ready, 1)

            low_w2(0)
            v.wait_ge(ld["b2"], 16)
            v.wait_ge(slotb_ready, 2)
            for e in range(E):
                if e:
                    outputs(e - 1)
                v.wait_ge(fhh_ready, e + 1)
                v.tensor_tensor(fhl[:], hT[:, e % 2], fhh[:].bitcast(F32), ALU.subtract).then_inc(fhl_ready, 1)
                v.tensor_scalar(selT[:, e, :], slotb[:], c_("slot0", e)[0:CAP], None, ALU.is_equal)\
                 .then_inc(selT_ready, 1)
                if e:
                    low_y(e - 1)
                if e + 1 < E:
                    low_w2(e + 1)
            outputs(E - 1)
            low_y(E - 1)
            for t in range(NT):
                v.wait_ge(comb_ps, t + 1)
                v.scalar_tensor_tensor(out=res[:, t, :], in0=ps[:, (6, 7, 0, 1, 2)[t], 0:D], scalar=s5[:, 1, t:t + 1],
                                       in1=h[:, t, :], op0=ALU.mult, op1=ALU.add).then_inc(res_ready, 1)

        @block.tensor
        def _(pe):
            def product(out_ap, terms):
                for i, (w, x) in enumerate(terms):
                    ins = pe.matmul(out_ap, w, x, start=(i == 0), stop=(i == len(terms) - 1), skip_group_check=True)
                return ins

            def split_terms(w_parts, x_parts):
                (wh, wl), (xh_, xl_) = w_parts, x_parts
                return [(wh, xh_), (wh, xl_), (wl, xh_)]

            def keep_warm(n):
                for _ in range(n):
                    pe.matmul(ps[:, 2, 0:P], onesm[:], onesm[:], start=True, stop=True,
                              skip_group_check=True)

            pe.wait_ge(consts, 2)
            keep_warm(WARM["start"])
            pe.wait_ge(ld["bz"], 16)
            for t in range(NT):
                pe.matmul(ps[:, Z_BANKS[t], 0:D], onesm[0:1, :], bz[:], start=True, stop=False, skip_group_check=True)
            keep_warm(WARM["patches"])
            pe.wait_ge(ld["idn"], 16)
            steps = [(g, i) for g in range(len(TOK_GROUPS)) for i in range(PC // 2)]
            for j in range(len(steps) + 3):
                if j >= 3:
                    g, i = steps[j - 3]
                    a, b = TOK_GROUPS[g]
                    pe.wait_ge(ld["wz"], 16)
                    pe.wait_ge(ztr_ready, j - 2)
                    for t in range(a, b):
                        for c in (2 * i, 2 * i + 1):
                            ins = pe.matmul(ps[:, Z_BANKS[t], 0:D], ztr[:, c, t * P:(t + 1) * P], wz[:, c, :],
                                            start=False, stop=(c == PC - 1), skip_group_check=True)
                        if i == PC // 2 - 1:
                            ins.then_inc(z_ps, 1)
                if j < len(steps):
                    g, i = steps[j]
                    a, b = TOK_GROUPS[g]
                    pe.wait_ge(pn_ready, b)
                    w = (b - a) * P
                    for c in (2 * i, 2 * i + 1):
                        for t in range(a, b):
                            ins = pe.transpose(ps[:, j % 3, (c % 2) * w + (t - a) * P:(c % 2) * w + (t - a + 1) * P],
                                               tok[:, t, c * P:(c + 1) * P], idn[:])
                    ins.then_inc(ztr_ps, 1)

            n_groups = [0]

            def xT_make(g):
                a, b = TOK_GROUPS[g]
                pe.wait_ge(xn_ready, n_groups[0] // len(TOK_GROUPS) * NT + b)
                w = (b - a) * P
                for c in range(KC):
                    for t in range(a, b):
                        ins = pe.transpose(ps[:, XT_BANKS[g], c * w + (t - a) * P:c * w + (t - a + 1) * P],
                                           xn[:, t, c * P:(c + 1) * P], idn[:])
                ins.then_inc(xT_ps, 1)
                n_groups[0] += 1

            def logits(g, w):
                pe.wait_ge(ld["gate"], 32)
                pe.wait_ge(xT_ready, (n_groups[0] - 1) // len(TOK_GROUPS) * len(TOK_GROUPS) + g + 1)
                for t in range(*TOK_GROUPS[g]):
                    ins = product(ps[:, 4, t * E:(t + 1) * E],
                                  [(xT[:, k, t * P:(t + 1) * P], w[:, k, :]) for k in range(KC)])
                if t == NT - 1:
                    ins.then_inc(lg_ps, 1)

            def attention(layer, w, wo, w_in, wo_in):
                xT_make(0)
                keep_warm(WARM["groups"][layer])
                xT_make(1)
                keep_warm(WARM["halves"][layer])
                pe.wait_ge(w_in, 16)
                for half in range(2):
                    pe.wait_ge(xT_ready, n_groups[0])
                    for i, base in enumerate((D, 0)):
                        if half == 0 and i == 1:
                            xT_make(2)
                        for m in range(KC):
                            product(ps[:, 4 * i + 2 * half + m, 0:HALF],
                                    [(w[:, k, base + m * P:base + (m + 1) * P],
                                      xT[:, k, half * HALF:(half + 1) * HALF]) for k in range(KC)]).then_inc(qk_ps, 1)

                def values_of(g):
                    pe.wait_ge(kT_ready, 4 * layer + g + 1)
                    for b in range(4 * g, 4 * g + 4):
                        for par in range(2):
                            c0 = 2 * D + par * P
                            ins = product(ps[par * SLOT:(par + 1) * SLOT, g, (b % 4) * P:(b % 4 + 1) * P],
                                          [(xT[:, k, b * T:b * T + SLOT], w[:, k, c0:c0 + P]) for k in range(KC)])
                    ins.then_inc(v_ps, 1)

                def projection(t):
                    pairs = NPAIR if t == NT - 1 else ceil((t + 1) * P / (2 * T))
                    pe.wait_ge(oT_ready, layer * NPAIR + pairs)
                    pe.wait_ge(s_shifted, layer * NPAIR + (NPAIR - 1 if t < 2 else NPAIR))
                    product(ps[:, Z_BANKS[t], 0:D],
                            [(oT[:, k, t * P:(t + 1) * P], wo[:, k, :]) for k in range(KC)]).then_inc(proj_ps, 1)

                values_of(0)
                pe.wait_ge(qT_ready, 4 * layer + 4)
                if layer == 0:
                    pe.wait_ge(consts, 6)
                pe.wait_ge(ld["masks"], 48)
                pe.wait_ge(wo_in, 16)
                for i in range(NPAIR + 4):
                    n = layer * NPAIR + i
                    if i < NPAIR:
                        if i >= 2:
                            pe.wait_ge(s_shifted, n - 1)
                        for m in range(KC):
                            if i in (0, NPAIR // 2):
                                pe.wait_ge(kbd_dve, 4 * layer + 4 * i // NPAIR + m + 1)
                                pe.wait_ge(kbd_pool, 4 * layer + 4 * i // NPAIR + m + 1)
                            bank = 4 + 2 * (i % 2) + m
                            if layer == 1:
                                pe.matmul(ps[:, bank, 0:HM * T], spreadm[:], bandm[:], start=True, stop=False,
                                          skip_group_check=True)
                            for j in range(2):
                                b = 2 * i + j
                                ins = pe.matmul(ps[j * SLOT:(j + 1) * SLOT, bank, 0:HM * T],
                                                qT[:, m, b * T:b * T + SLOT], kbd[:, m, :, b * T:(b + 1) * T],
                                                start=(layer == 0), stop=True, skip_group_check=True)
                        ins.then_inc(s_ps, 1)
                    if 1 <= i < 4:
                        values_of(i)
                    if NPAIR <= i < NPAIR + 2:
                        projection(i - NPAIR)
                    if 3 <= i < NPAIR + 3:
                        p = i - 3
                        pe.wait_ge(pn, n - 3 + 1)
                        if p == 0:
                            pe.wait_ge(vbd_ready, 8 * layer + 4)
                        else:
                            pe.wait_ge(pT_ready, n - 3)
                        for c in range(HM):
                            ins = pe.transpose(ps[:, c // 4, (c % 4) * P:(c % 4 + 1) * P],
                                               pe_[:, p % 4, 2 * c:2 * c + 2, :].rearrange("p h s -> p (h s)"), idn[:])
                        ins.then_inc(pT_ps, 1)
                    if i == NPAIR + 2:
                        projection(2)
                    if i >= 4:
                        p = i - 4
                        pe.wait_ge(pT_ready, n - 4 + 1)
                        if p == 0:
                            pe.wait_ge(vbd_ready, 8 * layer + 8)
                        if p >= 2:
                            pe.wait_ge(oT_ready, n - 4 - 1)
                        for j in range(2):
                            for c in range(HM):
                                q = slice(32 * (c % 4), 32 * (c % 4) + 32)
                                o = (c // 4) * 2 * T + j * T
                                ins = pe.matmul(ps[q, 2 + p % 2, o:o + T], vbd[:, 2 * p + j, c, :],
                                                pT[:, p % 2, c, j, :], start=True, stop=True, skip_group_check=True,
                                                tile_position=(0, 32 * (c % 4)))
                        ins.then_inc(o_ps, 1)
                projection(3)
                projection(4)
                xT_make(0)

            attention(0, wqkv0, wo0, ld["wqkv0"], ld["wo0"])

            def hidden_terms(n, m, half, low):
                for k in range(KC):
                    xs = xl if low else xh
                    for w_ in ((w1h,) if low else (w1h, w1l)):
                        ins = pe.matmul(ps[:, 2 * m + half, 0:HALF], w_[:, n % 2, k, m * P:(m + 1) * P],
                                        xs[:, k, half * HALF:(half + 1) * HALF],
                                        start=(k == 0 and w_ is w1h and not low), stop=(k == KC - 1 and low),
                                        skip_group_check=True)
                return ins

            def hidden_half(n, m, half):
                hidden_terms(n, m, half, False)
                return hidden_terms(n, m, half, True)

            def hidden(n):
                pe.wait_ge(w1h_ready, n + 1)
                pe.wait_ge(w1l_ready, n + 1)
                for m in range(KC):
                    pe.wait_ge(relu_ready, 2 * n - 1 + m)
                    hidden_half(n, m, 0)
                    hidden_half(n, m, 1).then_inc(hid_ps, 1)

            def outputs(n):
                pe.wait_ge(w2h_ready, n + 1)
                pe.wait_ge(w2l_ready, n + 1)
                pe.wait_ge(hl_ready, 2 * n + 2)
                for k, tiles in enumerate(Y_BANKS):
                    if n:
                        pe.wait_ge(y_used, 3 * (n - 1) + k + 1)
                    for t in tiles:
                        m = min(P, N - t * P)
                        ts = slice(t * P, t * P + m)
                        ins = product(ps[0:m, 5 + k, (t % 2) * D:(t % 2 + 1) * D],
                                      [x for c in range(KC) for x in split_terms(
                                          (hh[:, n % 2, c, ts], hl[:, n % 2, c, ts]),
                                          (w2h[:, n % 2, c, :], w2l[:, n % 2, c, :]))])
                    ins.then_inc(y_ps, 1)

            keep_warm(WARM["dense"])
            logits(0, gatew)
            xT_make(1)
            xT_make(2)
            pe.wait_ge(w1h_ready, 1)
            pe.wait_ge(w1l_ready, 1)
            for half in range(2):
                for low, ready in ((False, xh_ready), (True, xl_ready)):
                    pe.wait_ge(ready, half + 2)
                    if half:
                        pe.wait_ge(xT_ready, n_groups[0])
                    for m in range(KC):
                        ins = hidden_terms(0, m, half, low)
                        if low and half:
                            ins.then_inc(hid_ps, 1)
            logits(1, gatew)
            logits(2, gatew)
            for n in range(E + 1):
                if n < E:
                    hidden(n + 1)
                outputs(n)

            attention(1, wat1, wat1[:, :, 3 * D:4 * D], ld["wat1"], ld["wat1"])

            for g in range(len(TOK_GROUPS)):
                if g:
                    keep_warm(WARM["gate"])
                    xT_make(g)
                keep_warm(WARM["gate"])
                logits(g, wgw)
            keep_warm(WARM["top1"])
            pe.wait_ge(oh_ready, 1)
            for t in range(NT):
                ins = product(ps[:, 5, t * E:(t + 1) * E],
                              [(upperm[:, 1, :], ohb[:, s, :]) for s in range(t)] + [(upperm[:, 0, :], ohb[:, t, :])])
            ins.then_inc(cum_ps, 1)
            keep_warm(WARM["slots"])
            pe.wait_ge(tl_ready, 1)
            for t in range(NT):
                pe.wait_ge(sel_ready, t + 1)
                for j in range(4):
                    s, k = j // 2, j % 2
                    for part_ in (th, tl):
                        ins = pe.matmul(ps[:, j, 0:half_slots], part_[:, t, k * P:(k + 1) * P],
                                        sel[:, t, s * half_slots:(s + 1) * half_slots],
                                        start=(t == 0 and part_ is th), stop=(t == NT - 1 and part_ is tl),
                                        skip_group_check=True)
                    if t == NT - 1:
                        ins.then_inc(xg_ps, 1)
            for t in range(NT):
                pe.wait_ge(dg_ready, t + 1)
                ins = pe.matmul(ps[0:CAP, 6 + t // 4, (t % 4) * P:(t % 4 + 1) * P], onesm[:, 0:CAP], dg[:, t, :],
                                start=True, stop=True, skip_group_check=True)
                if t >= 3:
                    ins.then_inc(slotb_ps, 1)

            def up(e):
                pe.wait_ge(ld_f1[e % RING], 16 * (e // RING + 1))
                pe.wait_ge(xg_ready, 2 if e == 0 else 4)
                if e >= 2:
                    pe.wait_ge(gelu_ready, 2 * (e - 1))
                for q in range(2):
                    for f in range(4 * q, 4 * q + 4):
                        ins = product(ps[:, 2 * (e % 2) + q, (f % 4) * CAP:(f % 4 + 1) * CAP],
                                      [(fw1[:, e % RING, k, f * P:(f + 1) * P], xg[:, k, e * CAP:(e + 1) * CAP])
                                       for k in range(KC)])
                    ins.then_inc(fh_ps, 1)

            def down(e):
                pe.wait_ge(f2l_ready, e + 1)
                pe.wait_ge(fhl_ready, e + 1)
                if e >= 2:
                    pe.wait_ge(yt_ready, e - 1)
                product(ps[0:CAP, 4 + e % 2, 0:D],
                        [x for f in range(FC) for x in split_terms(
                            (fhh[:, f, :], fhl[:, f, :]), (f2h[:, e % 2, f, :], f2l[:, e % 2, f, :]))])\
                    .then_inc(fy_ps, 1)

            def combine(t, experts):
                for e in experts:
                    for part_ in (yh, yl):
                        ins = pe.matmul(ps[:, (6, 7, 0, 1, 2)[t], 0:D], selT[:, e, t * P:(t + 1) * P], part_[:, e, :],
                                        start=(e == 0 and part_ is yh), stop=(e == E - 1 and part_ is yl),
                                        skip_group_check=True)
                return ins

            up(0)
            for e in range(E):
                if e + 1 < E:
                    up(e + 1)
                else:
                    pe.wait_ge(yl_ready, E - 2)
                    for t in range(2):
                        combine(t, range(E - 2))
                down(e)
            pe.wait_ge(yl_ready, E - 1)
            pe.wait_ge(selT_ready, E)
            combine(2, range(E - 1))
            pe.wait_ge(yl_ready, E)
            for t in range(NT):
                combine(t, range((E - 2, E - 2, E - 1, 0, 0)[t], E)).then_inc(comb_ps, 1)


def layouts(x, cls_tok, L0_tok_ln1_g, L0_tok_ln1_b, L0_tok_W_proj, L0_tok_b_proj, L0_tok_ln2_g, L0_tok_ln2_b,
            L0_tok_cls_token, L0_tok_pos_emb, L0_attn_ln_gamma, L0_attn_ln_beta, L0_attn_W_qkv, L0_attn_b_qkv,
            L0_attn_W_proj, L0_attn_b_proj, L0_ffn_gate_w, L0_ffn_lb_bias, L0_ffn_w1, L0_ffn_w2, L0_ffn_cfc,
            L0_ffn_cproj, L1_attn_Wq, L1_attn_bq, L1_attn_Wk, L1_attn_bk, L1_attn_Wv, L1_attn_bv, L1_attn_Wo,
            L1_attn_bo, L1_ffn_wg, L1_ffn_W1, L1_ffn_b1, L1_ffn_W2, L1_ffn_b2):
    import numpy as np

    f32 = np.float32
    side = x.shape[2] // 6

    def by_token(a):
        a = np.concatenate([a.reshape(N, -1), np.zeros((NP - N, a.shape[-1]), f32)])
        return np.ascontiguousarray(a.reshape(NT, P, -1).transpose(1, 0, 2))

    def by_row(w):
        return np.ascontiguousarray(w.reshape(-1, P, w.shape[-1]).transpose(1, 0, 2))

    def by_col(a):
        return a.reshape(-1, P).T

    def odd_even(w):
        return w.reshape(w.shape[0], H // 2, 2, DH).transpose(0, 2, 1, 3).reshape(w.shape[0], D)

    pt = x.reshape(B, 3, 6, side, 6, side).transpose(0, 2, 4, 3, 5, 1).reshape(B, 36, PD)
    patches = by_token(np.concatenate([np.zeros((B, 2, PD), f32), pt], axis=1))
    wide = np.zeros((B, T, D), f32)
    scale_tok = wide.copy()
    scale_tok[:, 2:] = L0_tok_ln2_g
    shift_a = wide.copy()
    shift_a[:, 0] = cls_tok[0, 0]
    shift_a[:, 1:] = L0_tok_pos_emb[0]
    shift_b = wide.copy()
    shift_b[:, 1] = L0_tok_cls_token[0, 0]
    shift_b[:, 2:] = L0_tok_ln2_b
    w_qkv = by_row(np.concatenate([L0_attn_W_qkv[:, :2 * D], odd_even(L0_attn_W_qkv[:, 2 * D:])], axis=1))
    w_moe = np.stack([np.concatenate([by_row(a.T), by_row(b.T)], axis=1)
                      for a, b in [*zip(L0_ffn_w1, L0_ffn_w2), (L0_ffn_cfc, L0_ffn_cproj)]], axis=1)
    w_attn1 = by_row(np.concatenate([L1_attn_Wq.T, L1_attn_Wk.T, odd_even(L1_attn_Wv.T), L1_attn_Wo.T], axis=1))
    w1 = np.ascontiguousarray(L1_ffn_W1.reshape(E, KC, P, FF).transpose(2, 0, 1, 3))
    w2 = np.ascontiguousarray(L1_ffn_W2.reshape(E, FC, P, D).transpose(2, 0, 1, 3))
    bq0, bk0, bv0 = L0_attn_b_qkv.reshape(3, D)
    part = np.arange(P)
    head = (part[:, None] // DH == np.arange(HM)).astype(f32)
    slot0 = (part[:, None] + CAP * np.arange(E)).astype(f32)
    cols = np.concatenate([by_col(a) for a in (L0_tok_ln1_g, L0_tok_ln1_b, L0_attn_ln_gamma, L0_attn_ln_beta,
                                               bq0, bk0, bv0, L1_attn_bq, L1_attn_bk, L1_attn_bv, L1_ffn_b1)]
                          + [head, slot0], axis=1)
    rows = np.concatenate([L0_attn_b_proj, L1_attn_bo, L0_ffn_lb_bias, np.arange(E).astype(f32)])
    near = np.abs(np.arange(T)[:, None] - np.arange(T)[None, :]) <= 3
    band = np.tile(np.where(near, 0.0, -1e30).astype(f32), (1, HM))
    spread = np.zeros((T, 2, SLOT), f32)
    spread[:, :, :T] = np.eye(T, dtype=f32)[:, None, :]
    upper = np.stack([np.triu(np.ones((P, P), f32)), np.ones((P, P), f32)], axis=1)
    bf = np.dtype("bfloat16")
    return {
        "patches": patches, "scale_tok": by_token(scale_tok), "shift_a": by_token(shift_a),
        "shift_b": by_token(shift_b), "w_patch": by_row(L0_tok_W_proj), "w_qkv": w_qkv,
        "w_out": by_row(L0_attn_W_proj), "gate": by_row(L0_ffn_gate_w.T), "w_moe": np.ascontiguousarray(w_moe),
        "w_attn1": w_attn1, "wg": by_row(L1_ffn_wg), "w1": w1, "w2": w2, "cols": np.ascontiguousarray(cols),
        "rows": np.ascontiguousarray(np.broadcast_to(rows, (P, NROWS))),
        "b_patch": L0_tok_b_proj.reshape(1, D),
        "b2_rows": np.ascontiguousarray(np.broadcast_to(L1_ffn_b2, (P, E, D))),
        "iota_slots": np.ascontiguousarray(np.broadcast_to(np.arange(E * CAP, dtype=f32), (P, E * CAP))),
        "ident": np.eye(P, dtype=f32), "band": band.astype(bf), "spread": spread.reshape(T, P).astype(bf),
        "upper": upper.astype(bf),
    }


def kernel(**inputs):
    import numpy as np
    import concourse.bacc as bacc
    from concourse import mybir as mb
    from concourse.bass_utils import run_bass_kernel_spmd as run

    arrays = {f"in_{name}": a for name, a in layouts(**{k: np.asarray(v) for k, v in inputs.items()}).items()}
    nc = bacc.Bacc("TRN2", target_bir_lowering=False, num_devices=1)
    args = [nc.dram_tensor(name, a.shape, mb.dt.from_np(a.dtype), kind="ExternalInput").ap()
            for name, a in arrays.items()]
    result = nc.dram_tensor("out_0", (N, D), mb.dt.float32, kind="ExternalOutput").ap()
    vit_kernel(nc, *args, result)
    r = run(nc, [arrays], core_ids=[0])
    return r.results[0]["out_0"].reshape(B, T, D)
```
